# Optimizing a Trainium2 kernel written in Bass

```python
import numpy as np
import jax
import jax.numpy as jnp

def _softmax(x, axis=-1):
    return jax.nn.softmax(x, axis=axis)

def _gelu(x):
    return jax.nn.gelu(x, approximate=True)

def _silu(x):
    return jax.nn.silu(x)

def _sigmoid(x):
    return jax.nn.sigmoid(x)

def _layernorm(x, axis=-1, eps=1e-05):
    m = jnp.mean(x, axis=axis, keepdims=True)
    v = jnp.var(x, axis=axis, keepdims=True)
    return (x - m) / jnp.sqrt(v + eps)

def _scatter_add(tgt, idx, src, axis=0):
    return tgt.at[idx].add(src)

def _segment_sum(src, seg, n):
    return jax.ops.segment_sum(src, seg, n)
kernel_name = 'mk_xattn_seq_d4_seqx_r4_a7ee6d'

def setup_inputs(seed: int=0):
    np.random.seed(seed)
    _w = jnp.asarray

    def _rec_inputs():
        import jax
        import jax.numpy as jnp
        _rk = jax.random.key(seed)
        x = -0.0002928 + 1 * jax.random.normal(jax.random.fold_in(_rk, 1), (16, 100, 256), jnp.float32)
        _lenS = 100 - jax.random.randint(jax.random.fold_in(_rk, 7), (16,), 0, max(1, 100 // 4) + 1, jnp.int32)
        _lenS2 = 361 - jax.random.randint(jax.random.fold_in(_rk, 8), (16,), 0, max(1, 361 // 4) + 1, jnp.int32)
        _ctx_1024P = jax.random.normal(jax.random.fold_in(_rk, 11), (16, 16, 256), jnp.float32)
        _ctx_1024c = jax.random.dirichlet(jax.random.fold_in(_rk, 511), 0.3 * jnp.ones((16,), jnp.float32), (16, 361))
        _ctx_1024t = jnp.einsum('bsk,bkd->bsd', _ctx_1024c, _ctx_1024P)
        _ctx_1024t = _ctx_1024t * jax.lax.rsqrt(jnp.mean(jnp.square(_ctx_1024t)) + 1e-12) * 0.953939
        ctx_1024 = 4.13588e-05 + 0.999923 * (_ctx_1024t + 0.3 * jax.random.normal(jax.random.fold_in(_rk, 611), (16, 361, 256), jnp.float32))
        _validS = jnp.arange(100)[None, :] < _lenS[:, None]
        _validS2 = jnp.arange(361)[None, :] < _lenS2[:, None]
        _causal = jnp.tril(jnp.ones((100, 100), dtype=bool))
        mask_BxS2_bf1 = jnp.ones((16, 361), dtype=bool)
        return (x, ctx_1024, mask_BxS2_bf1)
    x, ctx_1024, mask_BxS2_bf1 = _rec_inputs()

    def _L0_xattn_setup():
        import jax, jax.numpy as jnp
        import numpy as np
        E = 256
        H = 16
        HD = E // H
        EPS = 1e-05

        def _layer_norm(x, g, b):
            mu = jnp.mean(x, axis=-1, keepdims=True)
            var = jnp.var(x, axis=-1, keepdims=True)
            return (x - mu) * jax.lax.rsqrt(var + EPS) * g + b
        key = jax.random.key(seed)
        ks = jax.random.split(key, 16)
        s = 0.02
        inp = {'query': jax.random.normal(ks[0], (4, 256, E), jnp.float32), 'key': jax.random.normal(ks[1], (4, 512, E), jnp.float32), 'value': jax.random.normal(ks[2], (4, 512, E), jnp.float32), 'wq': jax.random.normal(ks[3], (E, E), jnp.float32) * s, 'bq': jnp.zeros((E,), jnp.float32), 'wk': jax.random.normal(ks[4], (E, E), jnp.float32) * s, 'bk': jnp.zeros((E,), jnp.float32), 'wv': jax.random.normal(ks[5], (E, E), jnp.float32) * s, 'bv': jnp.zeros((E,), jnp.float32), 'wo': jax.random.normal(ks[6], (E, E), jnp.float32) * s, 'bo': jnp.zeros((E,), jnp.float32), 'ln1_g': jnp.ones((E,), jnp.float32), 'ln1_b': jnp.zeros((E,), jnp.float32), 'ln2_g': jnp.ones((E,), jnp.float32), 'ln2_b': jnp.zeros((E,), jnp.float32), 'w1': jax.random.normal(ks[7], (E, 4 * E), jnp.float32) * s, 'b1': jnp.zeros((4 * E,), jnp.float32), 'w2': jax.random.normal(ks[8], (4 * E, E), jnp.float32) * s, 'b2': jnp.zeros((E,), jnp.float32)}
        return inp
    _L0_xattn_all = _L0_xattn_setup()
    _L0_xattn_in = {k: v for k, v in _L0_xattn_all.items() if k in ('wq', 'bq', 'wk', 'bk', 'wv', 'bv', 'wo', 'bo', 'ln1_g', 'ln1_b', 'ln2_g', 'ln2_b', 'w1', 'b1', 'w2', 'b2')}
    del _L0_xattn_all

    def _L1_xattn_setup():
        import jax, jax.numpy as jnp
        import numpy as np
        B, Q, KV = (2, 512, 512)
        D_MODEL = 256
        N_HEADS = 16
        D_KV = 64
        EPS = 1e-06
        key = jax.random.key(seed)
        ks = jax.random.split(key, 7)
        s = 0.02
        return {'hidden_states': jax.random.normal(ks[0], (B, Q, D_MODEL), jnp.float32), 'key_value_states': jax.random.normal(ks[1], (B, KV, D_MODEL), jnp.float32), 'wq': jax.random.normal(ks[2], (D_MODEL, N_HEADS * D_KV), jnp.float32) * s, 'wk': jax.random.normal(ks[3], (D_MODEL, N_HEADS * D_KV), jnp.float32) * s, 'wv': jax.random.normal(ks[4], (D_MODEL, N_HEADS * D_KV), jnp.float32) * s, 'wo': jax.random.normal(ks[5], (N_HEADS * D_KV, D_MODEL), jnp.float32) * s, 'norm_w': jnp.ones((D_MODEL,), jnp.float32)}
    _L1_xattn_all = _L1_xattn_setup()
    _L1_xattn_in = {k: v for k, v in _L1_xattn_all.items() if k in ('wq', 'wk', 'wv', 'wo', 'norm_w')}
    del _L1_xattn_all

    def _L2_xattn_setup():
        import jax, jax.numpy as jnp
        import numpy as np
        NUM_HEADS = 16
        HEAD_DIM = 64
        D_MODEL = 256
        ROPE_BASE = 10000.0

        def rope(x):
            B, S, H, D = x.shape
            inv_freq = 1.0 / ROPE_BASE ** (jnp.arange(0, D, 2, dtype=jnp.float32) / D)
            t = jnp.arange(S, dtype=jnp.float32)
            freqs = jnp.einsum('s,d->sd', t, inv_freq)
            cos = jnp.cos(freqs)[None, :, None, :]
            sin = jnp.sin(freqs)[None, :, None, :]
            x1, x2 = (x[..., 0::2], x[..., 1::2])
            r1 = x1 * cos - x2 * sin
            r2 = x2 * cos + x1 * sin
            out = jnp.stack([r1, r2], axis=-1).reshape(B, S, H, D)
            return out.astype(x.dtype)
        key = jax.random.key(seed)
        ks = jax.random.split(key, 8)
        B, Sq, Skv = (4, 256, 512)
        d = D_MODEL
        hd = NUM_HEADS * HEAD_DIM
        scale = 1.0 / np.sqrt(d)
        return {'decoder_query': jax.random.normal(ks[0], (B, Sq, d), jnp.float32), 'encoder_key_value': jax.random.normal(ks[1], (B, Skv, d), jnp.float32), 'mask': jnp.ones((B, Skv), dtype=bool), 'Wq': jax.random.normal(ks[2], (d, hd), jnp.float32) * scale, 'Wk': jax.random.normal(ks[3], (d, hd), jnp.float32) * scale, 'Wv': jax.random.normal(ks[4], (d, hd), jnp.float32) * scale, 'Wo': jax.random.normal(ks[5], (hd, d), jnp.float32) * (1.0 / np.sqrt(hd)), 'ln_gamma': jnp.ones((d,), jnp.float32), 'ln_beta': jnp.zeros((d,), jnp.float32)}
    _L2_xattn_all = _L2_xattn_setup()
    _L2_xattn_in = {k: v for k, v in _L2_xattn_all.items() if k in ('Wq', 'Wk', 'Wv', 'Wo', 'ln_gamma', 'ln_beta')}
    del _L2_xattn_all

    def _L3_xattn_setup():
        import jax, jax.numpy as jnp
        import numpy as np
        DIM = 256
        N_HEADS = 16
        HEAD_DIM = DIM // N_HEADS
        LN_EPS = 1e-05

        def layer_norm(x, gamma, beta):
            mu = jnp.mean(x, axis=-1, keepdims=True)
            var = jnp.var(x, axis=-1, keepdims=True)
            return (x - mu) * jax.lax.rsqrt(var + LN_EPS) * gamma + beta
        key = jax.random.key(seed)
        ks = jax.random.split(key, 12)
        B, Nq, Nc, D = (2, 512, 512, DIM)
        s = 1.0 / np.sqrt(D)
        return {'query': jax.random.normal(ks[0], (B, Nq, D), jnp.float32), 'context': jax.random.normal(ks[1], (B, Nc, D), jnp.float32), 'Wq': jax.random.normal(ks[2], (D, D), jnp.float32) * s, 'bq': jnp.zeros((D,), jnp.float32), 'Wk': jax.random.normal(ks[3], (D, D), jnp.float32) * s, 'bk': jnp.zeros((D,), jnp.float32), 'Wv': jax.random.normal(ks[4], (D, D), jnp.float32) * s, 'bv': jnp.zeros((D,), jnp.float32), 'Wo': jax.random.normal(ks[5], (D, D), jnp.float32) * s, 'bo': jnp.zeros((D,), jnp.float32), 'gq': jnp.ones((D,), jnp.float32), 'betaq': jnp.zeros((D,), jnp.float32), 'gkv': jnp.ones((D,), jnp.float32), 'betakv': jnp.zeros((D,), jnp.float32)}
    _L3_xattn_all = _L3_xattn_setup()
    _L3_xattn_in = {k: v for k, v in _L3_xattn_all.items() if k in ('Wq', 'bq', 'Wk', 'bk', 'Wv', 'bv', 'Wo', 'bo', 'gq', 'betaq', 'gkv', 'betakv')}
    del _L3_xattn_all
    return {'x': x, 'ctx_1024': ctx_1024, 'mask_BxS2_bf1': mask_BxS2_bf1, 'L0_xattn_wq': _L0_xattn_in['wq'], 'L0_xattn_bq': _L0_xattn_in['bq'], 'L0_xattn_wk': _L0_xattn_in['wk'], 'L0_xattn_bk': _L0_xattn_in['bk'], 'L0_xattn_wv': _L0_xattn_in['wv'], 'L0_xattn_bv': _L0_xattn_in['bv'], 'L0_xattn_wo': _L0_xattn_in['wo'], 'L0_xattn_bo': _L0_xattn_in['bo'], 'L0_xattn_ln1_g': _L0_xattn_in['ln1_g'], 'L0_xattn_ln1_b': _L0_xattn_in['ln1_b'], 'L0_xattn_ln2_g': _L0_xattn_in['ln2_g'], 'L0_xattn_ln2_b': _L0_xattn_in['ln2_b'], 'L0_xattn_w1': _L0_xattn_in['w1'], 'L0_xattn_b1': _L0_xattn_in['b1'], 'L0_xattn_w2': _L0_xattn_in['w2'], 'L0_xattn_b2': _L0_xattn_in['b2'], 'L1_xattn_wq': _L1_xattn_in['wq'], 'L1_xattn_wk': _L1_xattn_in['wk'], 'L1_xattn_wv': _L1_xattn_in['wv'], 'L1_xattn_wo': _L1_xattn_in['wo'], 'L1_xattn_norm_w': _L1_xattn_in['norm_w'], 'L2_xattn_Wq': _L2_xattn_in['Wq'], 'L2_xattn_Wk': _L2_xattn_in['Wk'], 'L2_xattn_Wv': _L2_xattn_in['Wv'], 'L2_xattn_Wo': _L2_xattn_in['Wo'], 'L2_xattn_ln_gamma': _L2_xattn_in['ln_gamma'], 'L2_xattn_ln_beta': _L2_xattn_in['ln_beta'], 'L3_xattn_Wq': _L3_xattn_in['Wq'], 'L3_xattn_bq': _L3_xattn_in['bq'], 'L3_xattn_Wk': _L3_xattn_in['Wk'], 'L3_xattn_bk': _L3_xattn_in['bk'], 'L3_xattn_Wv': _L3_xattn_in['Wv'], 'L3_xattn_bv': _L3_xattn_in['bv'], 'L3_xattn_Wo': _L3_xattn_in['Wo'], 'L3_xattn_bo': _L3_xattn_in['bo'], 'L3_xattn_gq': _L3_xattn_in['gq'], 'L3_xattn_betaq': _L3_xattn_in['betaq'], 'L3_xattn_gkv': _L3_xattn_in['gkv'], 'L3_xattn_betakv': _L3_xattn_in['betakv']}

def reference(x, ctx_1024, mask_BxS2_bf1, L0_xattn_wq, L0_xattn_bq, L0_xattn_wk, L0_xattn_bk, L0_xattn_wv, L0_xattn_bv, L0_xattn_wo, L0_xattn_bo, L0_xattn_ln1_g, L0_xattn_ln1_b, L0_xattn_ln2_g, L0_xattn_ln2_b, L0_xattn_w1, L0_xattn_b1, L0_xattn_w2, L0_xattn_b2, L1_xattn_wq, L1_xattn_wk, L1_xattn_wv, L1_xattn_wo, L1_xattn_norm_w, L2_xattn_Wq, L2_xattn_Wk, L2_xattn_Wv, L2_xattn_Wo, L2_xattn_ln_gamma, L2_xattn_ln_beta, L3_xattn_Wq, L3_xattn_bq, L3_xattn_Wk, L3_xattn_bk, L3_xattn_Wv, L3_xattn_bv, L3_xattn_Wo, L3_xattn_bo, L3_xattn_gq, L3_xattn_betaq, L3_xattn_gkv, L3_xattn_betakv):
    import jax
    import jax.numpy as jnp

    def _L0_xattn_ref(query, key, value, wq, bq, wk, bk, wv, bv, wo, bo, ln1_g, ln1_b, ln2_g, ln2_b, w1, b1, w2, b2):
        import jax, jax.numpy as jnp
        import numpy as np
        E = 256
        H = 16
        HD = E // H
        EPS = 1e-05

        def _layer_norm(x, g, b):
            mu = jnp.mean(x, axis=-1, keepdims=True)
            var = jnp.var(x, axis=-1, keepdims=True)
            return (x - mu) * jax.lax.rsqrt(var + EPS) * g + b
        B, Sq, _ = query.shape
        Sk = key.shape[1]
        residual = query
        qn = _layer_norm(query, ln1_g, ln1_b)
        kn = _layer_norm(key, ln1_g, ln1_b)
        vn = _layer_norm(value, ln1_g, ln1_b)
        Q = (qn @ wq + bq).reshape(B, Sq, H, HD)
        K = (kn @ wk + bk).reshape(B, Sk, H, HD)
        V = (vn @ wv + bv).reshape(B, Sk, H, HD)
        scores = jnp.einsum('bqhd,bkhd->bhqk', Q, K) / jnp.sqrt(jnp.float32(HD))
        attn = jax.nn.softmax(scores, axis=-1)
        out = jnp.einsum('bhqk,bkhd->bqhd', attn, V).reshape(B, Sq, E)
        out = out @ wo + bo
        x = residual + out
        residual2 = x
        y = _layer_norm(x, ln2_g, ln2_b)
        y = jax.nn.gelu(y @ w1 + b1, approximate=False)
        y = y @ w2 + b2
        return residual2 + y

    def _L1_xattn_ref(hidden_states, key_value_states, wq, wk, wv, wo, norm_w):
        import jax, jax.numpy as jnp
        import numpy as np
        B, Q, KV = (2, 512, 512)
        D_MODEL = 256
        N_HEADS = 16
        D_KV = 64
        EPS = 1e-06
        var = jnp.mean(jnp.square(hidden_states), axis=-1, keepdims=True)
        normed = hidden_states * jax.lax.rsqrt(var + EPS) * norm_w
        b, q_len, _ = hidden_states.shape
        kv_len = key_value_states.shape[1]

        def split_heads(x):
            return x.reshape(b, -1, N_HEADS, D_KV).transpose(0, 2, 1, 3)
        q = split_heads(normed @ wq)
        k = split_heads(key_value_states @ wk)
        v = split_heads(key_value_states @ wv)
        scores = jnp.einsum('bhqd,bhkd->bhqk', q, k)
        attn = jax.nn.softmax(scores.astype(jnp.float32), axis=-1).astype(scores.dtype)
        ctx = jnp.einsum('bhqk,bhkd->bhqd', attn, v)
        ctx = ctx.transpose(0, 2, 1, 3).reshape(b, q_len, N_HEADS * D_KV)
        attn_out = ctx @ wo
        return hidden_states + attn_out

    def _L2_xattn_ref(decoder_query, encoder_key_value, mask, Wq, Wk, Wv, Wo, ln_gamma, ln_beta):
        import jax, jax.numpy as jnp
        import numpy as np
        NUM_HEADS = 16
        HEAD_DIM = 64
        D_MODEL = 256
        ROPE_BASE = 10000.0

        def rope(x):
            B, S, H, D = x.shape
            inv_freq = 1.0 / ROPE_BASE ** (jnp.arange(0, D, 2, dtype=jnp.float32) / D)
            t = jnp.arange(S, dtype=jnp.float32)
            freqs = jnp.einsum('s,d->sd', t, inv_freq)
            cos = jnp.cos(freqs)[None, :, None, :]
            sin = jnp.sin(freqs)[None, :, None, :]
            x1, x2 = (x[..., 0::2], x[..., 1::2])
            r1 = x1 * cos - x2 * sin
            r2 = x2 * cos + x1 * sin
            out = jnp.stack([r1, r2], axis=-1).reshape(B, S, H, D)
            return out.astype(x.dtype)
        B, Sq, d = decoder_query.shape
        Skv = encoder_key_value.shape[1]
        H, Dh = (NUM_HEADS, HEAD_DIM)
        q = (decoder_query @ Wq).reshape(B, Sq, H, Dh)
        k = (encoder_key_value @ Wk).reshape(B, Skv, H, Dh)
        v = (encoder_key_value @ Wv).reshape(B, Skv, H, Dh)
        q = rope(q)
        k = rope(k)
        q = q.transpose(0, 2, 1, 3) * (1.0 / jnp.sqrt(jnp.asarray(Dh, q.dtype)))
        k = k.transpose(0, 2, 1, 3)
        v = v.transpose(0, 2, 1, 3)
        scores = jnp.einsum('bhqd,bhkd->bhqk', q, k)
        m = mask[:, None, None, :]
        scores = jnp.where(m, scores, jnp.asarray(-1000000000.0, scores.dtype))
        attn = jax.nn.softmax(scores, axis=-1)
        out = jnp.einsum('bhqk,bhkd->bqhd', attn, v).reshape(B, Sq, H * Dh)
        out = out @ Wo
        x = decoder_query + out
        mu = jnp.mean(x, axis=-1, keepdims=True)
        var = jnp.var(x, axis=-1, keepdims=True)
        y = (x - mu) * jax.lax.rsqrt(var + 0.001) * ln_gamma + ln_beta
        return y

    def _L3_xattn_ref(query, context, Wq, bq, Wk, bk, Wv, bv, Wo, bo, gq, betaq, gkv, betakv):
        import jax, jax.numpy as jnp
        import numpy as np
        DIM = 256
        N_HEADS = 16
        HEAD_DIM = DIM // N_HEADS
        LN_EPS = 1e-05

        def layer_norm(x, gamma, beta):
            mu = jnp.mean(x, axis=-1, keepdims=True)
            var = jnp.var(x, axis=-1, keepdims=True)
            return (x - mu) * jax.lax.rsqrt(var + LN_EPS) * gamma + beta
        B, Nq, D = query.shape
        Nc = context.shape[1]
        residual = query
        q = layer_norm(query, gq, betaq)
        c = layer_norm(context, gkv, betakv)
        Q = (q @ Wq + bq).reshape(B, Nq, N_HEADS, HEAD_DIM).transpose(0, 2, 1, 3)
        K = (c @ Wk + bk).reshape(B, Nc, N_HEADS, HEAD_DIM).transpose(0, 2, 1, 3)
        V = (c @ Wv + bv).reshape(B, Nc, N_HEADS, HEAD_DIM).transpose(0, 2, 1, 3)
        scores = jnp.einsum('bhqd,bhkd->bhqk', Q, K) / np.sqrt(HEAD_DIM).astype(np.float32)
        attn = jax.nn.softmax(scores, axis=-1)
        out = jnp.einsum('bhqk,bhkd->bhqd', attn, V)
        out = out.transpose(0, 2, 1, 3).reshape(B, Nq, D)
        return residual + out @ Wo + bo
    x = _L0_xattn_ref(x, ctx_1024, ctx_1024, L0_xattn_wq, L0_xattn_bq, L0_xattn_wk, L0_xattn_bk, L0_xattn_wv, L0_xattn_bv, L0_xattn_wo, L0_xattn_bo, L0_xattn_ln1_g, L0_xattn_ln1_b, L0_xattn_ln2_g, L0_xattn_ln2_b, L0_xattn_w1, L0_xattn_b1, L0_xattn_w2, L0_xattn_b2)
    x = _L1_xattn_ref(x, ctx_1024, L1_xattn_wq, L1_xattn_wk, L1_xattn_wv, L1_xattn_wo, L1_xattn_norm_w)
    x = _L2_xattn_ref(x, ctx_1024, mask_BxS2_bf1, L2_xattn_Wq, L2_xattn_Wk, L2_xattn_Wv, L2_xattn_Wo, L2_xattn_ln_gamma, L2_xattn_ln_beta)
    x = _L3_xattn_ref(x, ctx_1024, L3_xattn_Wq, L3_xattn_bq, L3_xattn_Wk, L3_xattn_bk, L3_xattn_Wv, L3_xattn_bv, L3_xattn_Wo, L3_xattn_bo, L3_xattn_gq, L3_xattn_betaq, L3_xattn_gkv, L3_xattn_betakv)
    return x

_drawn_inputs = setup_inputs


def setup_inputs(seed=0):
    import zlib

    import numpy as np

    out = dict(_drawn_inputs(seed))
    spreads = {'L0_xattn_bq': (0.0, 0.8),
     'L0_xattn_bk': (0.0, 0.8),
     'L0_xattn_bv': (0.0, 0.316),
     'L0_xattn_bo': (0.0, 0.1),
     'L0_xattn_ln1_g': (1.0, 0.6),
     'L0_xattn_ln1_b': (0.0, 0.8),
     'L0_xattn_ln2_g': (1.0, 0.6),
     'L0_xattn_ln2_b': (0.0, 0.8),
     'L0_xattn_b1': (0.0, 0.339),
     'L0_xattn_b2': (0.0, 0.1),
     'L1_xattn_norm_w': (1.0, 0.6),
     'L2_xattn_ln_gamma': (1.0, 0.2),
     'L2_xattn_ln_beta': (0.0, 0.1),
     'L3_xattn_bq': (0.0, 0.519),
     'L3_xattn_bk': (0.0, 0.8),
     'L3_xattn_bv': (0.0, 0.1),
     'L3_xattn_bo': (0.0, 0.1),
     'L3_xattn_gq': (1.0, 0.2),
     'L3_xattn_betaq': (0.0, 0.497),
     'L3_xattn_gkv': (1.0, 0.2),
     'L3_xattn_betakv': (0.0, 0.1)}
    factors = {'L0_xattn_wq': 8.0, 'L0_xattn_wk': 8.0}
    for name, (base, spread) in spreads.items():
        noise = np.random.default_rng([zlib.crc32(name.encode()), seed]).standard_normal(out[name].shape)
        drawn = base * np.exp(spread * noise) if base else spread * noise
        out[name] = jnp.asarray(drawn.astype(out[name].dtype))
    for name, factor in factors.items():
        out[name] = (out[name] * factor).astype(out[name].dtype)
    return out
```

```python
import concourse.bass as bass
from concourse import mybir
from contextlib import ExitStack

fp32 = mybir.dt.float32
f32r = mybir.dt.float32r
u8 = mybir.dt.uint8
ALU = mybir.AluOpType
ACT = mybir.ActivationFunctionType
AX = mybir.AxisListType

B, SQ, SK, E, H = 16, 100, 361, 256, 16
KE = E // 128
KV_TILES = -(-SK // 128)
KV_ROWS = [min(128, SK - 128 * t) for t in range(KV_TILES)]
SKP = 128 * KV_TILES
SKE = SK + SK % 2
PAIRS = B // 2
FF = 4 * E
NEG = 1.0e9

C_ID, C_COS, C_SIN, C_NEG, C_FILL, C_END = 0, 128, 128 + SKE, 128 + 2 * SKE, 129 + 2 * SKE, 129 + 2 * SKE + SQ


VEC_COLS, VEC_END = {}, 0
for _p in ("L0", "L3"):
    for _v, _n in (("cg", KE), ("cb", KE), ("xg", KE), ("xb", KE), ("bq", 4), ("bk", 4), ("bv", 4)):
        VEC_COLS[_p + _v], VEC_END = VEC_END, VEC_END + _n
for _v, _n in (("g2", KE), ("b2n", KE), ("b1", FF // 128), ("nw", KE)):
    VEC_COLS[_v], VEC_END = VEC_END, VEC_END + _n


class Layer:

    def __init__(self, name, hd, ctx_norm, x_norm, rope, eps, eps_post=None):
        self.name, self.hd, self.ctx_norm, self.x_norm, self.rope = name, hd, ctx_norm, x_norm, rope
        self.eps, self.eps_post = eps, eps_post
        self.wide = hd == 64
        self.rows = 64 if self.wide else 32
        self.per = 128 // self.rows
        self.nt = H // self.per
        self.hw = self.rows * H
        self.vn = 512 if self.wide else 256
        self.nv = KV_TILES * (hd * H // self.vn)
        self.nr = -(-self.nt // 4)
        self.half = self.nt // 2


class Steps:

    def __init__(self, keys, base, parity=0):
        self.at = {k: n for n, k in enumerate(keys)}
        assert len(self.at) == len(keys)
        self.base, self.parity, self.count = base, parity, len(keys)

    def upto(self, key):
        return self.base + (self.at[key] + 1)

    def slot(self, key):
        return (self.parity + self.at[key]) % 2

    def before(self, u):
        return self.base + sum(1 for k in self.at if k[1] < u)


class Stage:

    def __init__(self, L, i, last=False):
        self.i, self.last, self.first = i, last, isinstance(i, int) and i < 0
        jobs0 = self.jobs_of(L, -1, False)
        jobs1 = self.jobs_of(L, 0, False)
        splits0, splits1 = [[k for k in j if k[0] in ("ctx", "K", "xT", "Q")] for j in (jobs0, jobs1)]
        norms0, norms1 = self.norms_of(L, -1, False), self.norms_of(L, 0, False)
        assert len(jobs1) % 2 == 0 and len(splits1) % 2 == 0
        jobs = self.jobs_of(L, -1 if self.first else 0, last)
        splits = [k for k in jobs if k[0] in ("ctx", "K", "xT", "Q")]
        norms = self.norms_of(L, -1 if self.first else 0, last)

        def base(a, b):
            return 0 if self.first else len(a) + i * len(b)
        self.jobs = Steps(jobs, base(jobs0, jobs1), 0 if self.first else len(jobs0) % 2)
        self.splits = Steps(splits, base(splits0, splits1), 0 if self.first else len(splits0) % 2)
        self.norms = Steps(norms, base(norms0, norms1))
        turns0, turns1, turns = [[k for k in j if k[0] in "KQ"] for j in (jobs0, jobs1, jobs)]
        assert len(turns1) % 2 == 0
        self.turns = Steps(turns, base(turns0, turns1), 0 if self.first else len(turns0) % 2)

    def has_next(self, u):
        return not (self.last and u == 1)

    def has_pair(self, u):
        return self.first or (u == 1 and not self.last)

    @staticmethod
    def jobs_of(L, i, last):
        out = []
        for u in ([-1] if i < 0 else [0, 1]):
            nxt = i < 0 or not (last and u == 1)
            pair = i < 0 or (u == 1 and not last)
            if nxt:
                out += [("ctx", u, k) for k in range(KE)]
            if pair:
                out += [("xT", u, k) for k in range(KE)]
            if nxt:
                out += [("K", u, t) for t in range(L.half)]
            if i >= 0:
                out += [("R", u, r) for r in range(L.nr)]
            if nxt:
                out += [("K", u, t) for t in range(L.half, L.nt)]
            if pair:
                out += [("Q", u, t) for t in range(L.nt)]
            if i >= 0:
                out += [("out", u, 0)]
            if nxt:
                out += [("V", u, c) for c in range(L.nv)]
        return out

    @staticmethod
    def norms_of(L, i, last):
        out = []
        for u in ([-1] if i < 0 else [0, 1]):
            if L.ctx_norm and (i < 0 or not (last and u == 1)):
                out.append(("ctx", u))
            if L.x_norm and (i < 0 or (u == 1 and not last)):
                out.append(("x", u))
            if L.eps_post is not None and i >= 0:
                out.append(("post", u))
        return out

    def pair(self):
        return 1 if self.first else self.i + 2

    def batch(self, u):
        return self.i * 2 + u

    def head(self, u, h):
        return self.i * (2 * H) + (H * u + h + 1)


PASSED = []


def wait_apart(eng, s, value):
    eng.wait_ge(s, value)
    eng.sem_inc(PASSED[0], 1)


def build(nc, a, consts, out):
    stack = ExitStack()
    with stack:
        def sb(name, shape, dt=fp32):
            return stack.enter_context(nc.sbuf_tensor(name, shape, dt))

        def ps(name, shape):
            return stack.enter_context(nc.psum_tensor(name, shape, fp32))

        def sem(name):
            return stack.enter_context(nc.semaphore(name))

        X = sb("X", [SQ, B, E])
        CON = sb("CON", [128, C_END])
        ident = CON[:, C_ID:C_ID + 128]
        cos, sin = CON[:, C_COS:C_COS + SKE], CON[:, C_SIN:C_SIN + SKE]
        low_half = CON[:, C_NEG:C_NEG + 1]
        VEC = sb("VEC", [128, VEC_END])
        ROWS = sb("ROWS", [SQ, 5, E])
        W_RAW = sb("W_RAW", [128, 3, 2048])
        WH = sb("WH", [128, 6144], f32r)
        WL = sb("WL", [128, 6144], f32r)
        WO = sb("WO", [128, 2048])
        C = sb("C", [128, 2, KV_TILES, E])
        CTH, CTL = sb("CTH", [128, KE, SKE], f32r), sb("CTL", [128, KE, SKE], f32r)
        KH, KL = sb("KH", [128, 8, SKE], f32r), sb("KL", [128, 8, SKE], f32r)
        KR = KL[:, 0:2, :]
        V = sb("V", [128, 3200])
        QH, QL = sb("QH", [128, 8, 2 * SQ], f32r), sb("QL", [128, 8, 2 * SQ], f32r)
        T32 = sb("T32", [128, 2, 4 * SQ])
        WORK = sb("WORK", [128, 7 * SKE])
        CN = WORK[:, 0:KV_TILES * E].rearrange("p (t e) -> p t e", e=E)
        SH, AC = [WORK[:, n * SKE:(n + 2) * SKE].rearrange("p (s n) -> p s n", s=2) for n in (0, 2)]
        COSM, SINM, MF = [WORK[:, n * SKE:(n + 1) * SKE] for n in (4, 5, 6)]
        M8 = sb("M8", [128, 2, SKE], u8)
        MNEG = sb("MNEG", [2, 2, SKE], f32r)
        FILL = sb("FILL", [2, SQ], f32r)
        XN = sb("XN", [SQ, 2, E])
        XTH, XTL = sb("XTH", [128, KE, 2 * SQ], f32r), sb("XTL", [128, KE, 2 * SQ], f32r)
        P = sb("P", [SQ, 4, SKP])
        PT = sb("PT", [128, 2, KV_TILES * SQ])
        RX = sb("RX", [SQ, H * 64])
        OT = sb("OT", [128, 8, SQ])
        Y = sb("Y", [SQ, E])
        MX = sb("MX", [SQ, 2, H])
        DEN = sb("DEN", [SQ, 2, H])
        RDEN = sb("RDEN", [SQ, H])
        BN = sb("BN", [128, 4, 6])
        MV = sb("MV", [128, 4, 2])
        VE = sb("VE", [128, 4])
        EV = sb("EV", [128, 4])
        SQV = sb("SQV", [128, 4])
        RS = sb("RS", [128, 4])
        HALF = sb("HALF", [128, 4])

        PJ = [ps(f"PJ{n}", [128, 512]) for n in range(2)]
        PS_ = [ps(f"PS{n}", [128, 512]) for n in range(2)]
        PP = [ps(f"PP{n}", [128, 512]) for n in range(2)]
        PO = [ps(f"PO{n}", [128, 512]) for n in range(2)]

        def col(name, k=0):
            c = VEC_COLS[name] + k
            return VEC[:, c:c + 1]

        LAYERS = [Layer("L0", 16, True, True, False, 1e-5), Layer("L1", 64, False, True, False, 1e-6),
                  Layer("L2", 64, False, False, True, None, 1e-3), Layer("L3", 16, True, True, False, 1e-5)]
        PHASES = [LAYERS[0], "ffn", LAYERS[1], LAYERS[2], LAYERS[3]]
        names = ["L0", "ffn", "L1", "L2", "L3"]
        w_in = {n: [sem(f"{n}_w{c}_in") for c in range(3)] for n in names}
        wo_in = {n: sem(f"{n}_wo_in") for n in names}
        wo_parts = {"L0": 64, "ffn": 16, "L1": 16, "L2": 16, "L3": 64}

        def raw(c, n):
            return W_RAW[:, c, 0:KE * n].rearrange("p (k n) -> p k n", k=KE)

        def load_weights(eng, n):
            if n == "ffn":
                eng.dma_start(raw(0, FF), a["L0_xattn_w1"].rearrange("(k p) n -> p k n", p=128)).then_inc(w_in[n][0], 16)
                return
            up = {"L0": "L0_xattn_w", "L1": "L1_xattn_w", "L2": "L2_xattn_W", "L3": "L3_xattn_W"}[n]
            width = 1024 if n in ("L1", "L2") else E
            for c, which in enumerate("kvq"):
                eng.dma_start(raw(c, width), a[up + which].rearrange("(k p) n -> p k n", p=128)).then_inc(w_in[n][c], 16)

        def load_output_weights(eng, n):
            if n == "ffn":
                src = a["L0_xattn_w2"]
            elif n in ("L1", "L2"):
                src = a["L1_xattn_wo" if n == "L1" else "L2_xattn_Wo"]
            else:
                src = a[n + ("_xattn_wo" if n == "L0" else "_xattn_Wo")].rearrange("(t g p) n -> g p t n", g=4, p=16)
                for g in range(4):
                    eng.dma_start(WO[32 * g:32 * g + 16, 0:4 * E].rearrange("p (t n) -> p t n", t=4),
                                  src[g]).then_inc(wo_in[n], 16)
                return
            eng.dma_start(WO[:, :].rearrange("p (t n) -> p t n", t=8),
                          src.rearrange("(t p) n -> p t n", p=128)).then_inc(wo_in[n], 16)

        def load_context(eng, n, slot, s_in):
            eng.dma_start(C[:, slot, 0:2, :], a["ctx_1024"][n, 0:256, :].rearrange("(t p) f -> p t f", p=128)).then_inc(s_in[slot], 16)
            eng.dma_start(C[0:KV_ROWS[2], slot, 2, :], a["ctx_1024"][n, 256:SK, :]).then_inc(s_in[slot], 16)

        s_con, s_x, s_vec, s_rows = sem("con_in"), sem("x_in"), sem("vectors_in"), sem("rows_in")
        with nc.Block() as block:
            row_src = ["L0_xattn_bo", "L0_xattn_b2", "L2_xattn_ln_gamma", "L2_xattn_ln_beta", "L3_xattn_bo"]

            @block.sync
            def _(eng):
                load_weights(eng, "L0")
                eng.dma_start(X[:, :, :], a["x"].rearrange("b s f -> s b f")).then_inc(s_x, 16)
                for r, src in enumerate(row_src):
                    eng.dma_start(ROWS[:, r, :], a[src].rearrange("(o n) -> o n", o=1).broadcast_to([SQ, E])).then_inc(s_rows, 16)
                eng.wait_ge(s_rows, 16 * len(row_src))
                eng.wait_ge(s_x, 16)

            @block.scalar
            def _(eng):
                eng.dma_start(CON[:, :], consts).then_inc(s_con, 16)
                eng.dma_start(VEC[:, :], a["vectors"]).then_inc(s_vec, 16)
                eng.wait_ge(s_vec, 16)
                eng.wait_ge(s_con, 16)

            @block.vector
            def _(eng):
                eng.memset(HALF[:, :], -0.5)
                eng.memset(MV[:, :, :], 1.0)
                eng.memset(M8[:, :, SK:SKE], 0)
                for half in (CTH, CTL):
                    eng.memset(half[:, :, SK:SKE].bitcast(fp32), 0.0)
                eng.memset(P[:, :, SK:SKP], 0.0)
                eng.wait_ge(s_con, 16)
                eng.tensor_copy(FILL[:, :], CON[0:2, C_FILL:C_FILL + SQ])

        PASSED[:] = [sem("passed")]
        S = {k: sem(k) for k in
                 ("high_w", "low_w", "cleared_v", "cleared_w",
                  "product",
                  "taken",
                  "rounded",
                  "split",
                  "scores", "maxed", "exped",
                  "turned", "unloaded", "weighed",
                  "inverse", "repeated",
                  "scaled", "freed", "added", "summed",
                  "stats", "moments", "square", "squares", "powers", "rstd", "normed",
                  "copied", "shuffled", "rotated", "joined", "mask_float", "mask_tables", "gammaed")}
        s_c = [sem(f"context{n}_in") for n in range(2)]
        s_m = [sem(f"mask{n}_in") for n in range(2)]
        s_out = sem("out_written")

        def clear_semaphores():
            with nc.Block() as block:

                @block.sync
                def _(sp):
                    for s in [*S.values(), *s_c, *s_m, *PASSED]:
                        sp.sem_clear(s)

        def attention(L, ph):
            nm = L.name
            n_ = KE * L.hw
            wk, wv, wq = 0, n_, n_ + KE * L.hd * H
            vw = L.hd * H

            def wcols(c):
                at, w = ((wk, L.hw), (wv, vw), (wq, L.hw))[c]
                return at, w

            def wsplit(W, c):
                at, w = wcols(c)
                ap = W[:, at:at + KE * w]
                if L.wide or c == 1:
                    return ap
                return ap.rearrange("p (m d e) -> p m d e", d=2, e=16)

            def wraw(c):
                ap = W_RAW[:, c, 0:KE * vw]
                if L.wide or c == 1:
                    return ap
                return ap.rearrange("p (m e) -> p m e", e=16).unsqueeze(2).to_broadcast([128, KE * H, 2, 16])

            def w(W, c, k, n0, n1):
                at, width = wcols(c)
                return W[:, at + k * width + n0:at + k * width + n1]

            def loop(eng, body):
                with eng.Fori(0, PAIRS - 1) as i:
                    body(Stage(L, i))
                body(Stage(L, PAIRS - 1, last=True))

            with nc.Block() as block:

                @block.sync
                def _(sp):
                    for n in range(2):
                        load_context(sp, n, n, s_c)
                        if L.rope:
                            sp.dma_start(M8[:, n, 0:SK], a["mask"][n:n + 1, :].broadcast_to([128, SK])).then_inc(s_m[n], 16)
                    if not L.wide:
                        sp.wait_ge(S["cleared_w"], 1)
                    load_output_weights(sp, nm)
                    if ph < 4:
                        sp.wait_ge(S["low_w"], 3)
                        load_weights(sp, names[ph + 1])

                    def body(st):
                        for u in range(2):
                            if st.last:
                                continue
                            wait_apart(sp, S["scores"], st.head(u, 0))
                            load_context(sp, st.batch(u) + 2, u, s_c)
                            if L.rope:
                                wait_apart(sp, S["mask_tables"], st.batch(u) + 1)
                                n = st.batch(u) + 2
                                sp.dma_start(M8[:, u, 0:SK], a["mask"][bass.ds(n, 1), :].broadcast_to([128, SK])).then_inc(s_m[u], 16)
                    loop(sp, body)
                    if ph == 4:
                        sp.wait_ge(S["summed"], B)
                        sp.dma_start(out.rearrange("b s f -> s b f"), X[:, :, :]).then_inc(s_out, 16)
                        sp.wait_ge(s_out, 16)

                @block.tensor
                def _(pe):
                    pe.sem_inc(S["turned"], 4)
                    pe.sem_inc(S["weighed"], 2)

                    def begin(st, key):
                        j = st.jobs.upto(key)
                        if not isinstance(j, int) or j > 2:
                            pe.wait_ge(S["taken"], j - 2)
                        return PJ[st.jobs.slot(key)]

                    def product3(dst, pairs):
                        todo = [x for lh, ll, rh, rl in pairs for x in ((lh, rh), (lh, rl), (ll, rh))]
                        for n, (l, r) in enumerate(todo):
                            last = nc.tensor.matmul(dst, l, r, start=n == 0, stop=n == len(todo) - 1)
                        return last

                    def context_turn(st, u, n):
                        if L.ctx_norm:
                            pe.wait_ge(S["normed"], st.norms.upto(("ctx", u)))
                        else:
                            pe.wait_ge(s_c[n % 2], 32 if st.first else st.i * 32 + 32 * (u + 1))
                        src = CN if L.ctx_norm else C[:, n % 2]
                        for k in range(KE):
                            bank = begin(st, ("ctx", u, k))
                            for t, r in enumerate(KV_ROWS):
                                last = nc.tensor.transpose(bank[:, 128 * t:128 * t + r], src[0:r, t, 128 * k:128 * k + 128], ident[0:r, 0:r])
                            last.then_inc(S["product"], 1)

                    def keys(st, u, t0, t1):
                        pe.wait_ge(S["split"], st.splits.upto(("ctx", u, KE - 1)))
                        for t in range(t0, t1):
                            bank = begin(st, ("K", u, t))
                            product3(bank[:, 0:SKE], [(w(WH, 0, k, 128 * t, 128 * t + 128), w(WL, 0, k, 128 * t, 128 * t + 128),
                                                      CTH[:, k, :], CTL[:, k, :]) for k in range(KE)]).then_inc(S["product"], 1)

                    def values(st, u):
                        for c in range(L.nv):
                            t, part = c % KV_TILES, c // KV_TILES
                            r = KV_ROWS[t]
                            bank = begin(st, ("V", u, c))
                            product3(bank[0:r, 0:L.vn],
                                     [(CTH[:, k, 128 * t:128 * t + r], CTL[:, k, 128 * t:128 * t + r],
                                       w(WH, 1, k, L.vn * part, L.vn * part + L.vn), w(WL, 1, k, L.vn * part, L.vn * part + L.vn))
                                      for k in range(KE)]).then_inc(S["product"], 1)

                    def query_turn(st, u):
                        if L.x_norm:
                            pe.wait_ge(S["normed"], st.norms.upto(("x", u)))
                        else:
                            pe.wait_ge(S["copied"], st.pair())
                        for k in range(KE):
                            bank = begin(st, ("xT", u, k))
                            for v in range(2):
                                last = nc.tensor.transpose(bank[:, SQ * v:SQ * v + SQ], XN[:, v, 128 * k:128 * k + 128], ident[0:SQ, 0:SQ])
                            last.then_inc(S["product"], 1)

                    def queries(st, u):
                        pe.wait_ge(S["split"], st.splits.upto(("xT", u, KE - 1)))
                        for t in range(L.nt):
                            bank = begin(st, ("Q", u, t))
                            product3(bank[:, 0:2 * SQ], [(w(WH, 2, k, 128 * t, 128 * t + 128), w(WL, 2, k, 128 * t, 128 * t + 128),
                                                          XTH[:, k, :], XTL[:, k, :]) for k in range(KE)]).then_inc(S["product"], 1)

                    def heads(st, u):
                        pe.wait_ge(S["split"], st.splits.before(u))
                        if L.rope:
                            pe.wait_ge(S["mask_tables"], st.batch(u) + 1)
                        for s in range(H + 3):
                            if s < H:
                                h, t, r0 = s, s // L.per, L.rows * (s % L.per)
                                pe.wait_ge(S["exped"], st.head(u, h))
                                q = slice(SQ * u, SQ * u + SQ)
                                qh, ql = QH[r0:r0 + L.rows, t, q], QL[r0:r0 + L.rows, t, q]
                                kh, kl = KH[r0:r0 + L.rows, t, :], KL[r0:r0 + L.rows, t, :]
                                todo = [(qh, kh), (qh, kl), (ql, kh)] if L.wide else [(qh, kh), (ql, kh)]
                                if L.rope:
                                    todo = [(FILL[:, :], MNEG[:, u, :])] + todo
                                for n, (x, y) in enumerate(todo):
                                    last = nc.tensor.matmul(PS_[h % 2][0:SQ, 0:SKE], x, y, start=n == 0, stop=n == len(todo) - 1)
                                last.then_inc(S["scores"], 1)
                            if 2 <= s < H + 2:
                                h = s - 2
                                pe.wait_ge(S["exped"], st.head(u, h) + 2)
                                pe.wait_ge(S["unloaded"], st.head(u, h))
                                for t in range(KV_TILES):
                                    last = nc.tensor.transpose(PP[h % 2][:, SQ * t:SQ * t + SQ], P[:, h % 4, 128 * t:128 * t + 128], ident[0:SQ, 0:SQ])
                                last.then_inc(S["turned"], 1)
                            if s >= 3:
                                h = s - 3
                                t, r0 = h // L.per, L.rows * (h % L.per)
                                if h == 0:
                                    pe.wait_ge(S["taken"], st.jobs.before(u))
                                    pe.wait_ge(S["freed"], (st.batch(u) + 1) * L.nr)
                                pe.wait_ge(S["unloaded"], st.head(u, h) + 2)
                                for c, r in enumerate(KV_ROWS):
                                    last = nc.tensor.matmul(PO[t // 4][r0:r0 + L.rows, SQ * (t % 4):SQ * (t % 4) + SQ],
                                                            V[0:r, c * L.hw + L.rows * h:c * L.hw + L.rows * h + L.rows],
                                                            PT[0:r, h % 2, SQ * c:SQ * c + SQ], start=c == 0, stop=c == KV_TILES - 1)
                                last.then_inc(S["weighed"], 1)
                            if s == 10 and st.has_next(u):
                                context_turn(st, u, 1 - u)

                    def spread(st, u):
                        pe.wait_ge(S["repeated"], st.batch(u) + 1)
                        for r in range(L.nr):
                            bank = begin(st, ("R", u, r))
                            for t in range(4):
                                c = 128 * (4 * r + t)
                                last = nc.tensor.transpose(bank[:, SQ * t:SQ * t + SQ], RX[:, c:c + 128], ident[0:SQ, 0:SQ])
                            last.then_inc(S["product"], 1)

                    def project(st, u):
                        bank = begin(st, ("out", u, 0))
                        pe.wait_ge(S["scaled"], st.batch(u) + 1)
                        for t in range(L.nt):
                            last = nc.tensor.matmul(bank[0:SQ, 0:E], OT[:, t, :], WO[:, E * t:E * t + E], start=t == 0, stop=t == L.nt - 1)
                        last.then_inc(S["product"], 1)

                    st = Stage(L, -1)
                    context_turn(st, -1, 0)
                    query_turn(st, -1)
                    pe.wait_ge(S["low_w"], 1)
                    keys(st, -1, 0, L.nt)
                    pe.wait_ge(S["low_w"], 3)
                    queries(st, -1)
                    values(st, -1)
                    pe.wait_ge(wo_in[nm], wo_parts[nm])

                    def body(st):
                        for u in range(2):
                            heads(st, u)
                            if st.has_pair(u):
                                query_turn(st, u)
                            if st.has_next(u):
                                keys(st, u, 0, L.half)
                            spread(st, u)
                            if st.has_next(u):
                                keys(st, u, L.half, L.nt)
                            if st.has_pair(u):
                                queries(st, u)
                            project(st, u)
                            if st.has_next(u):
                                values(st, u)
                    loop(pe, body)

                @block.scalar
                def _(act):
                    act.sem_inc(S["exped"], 2)

                    def split_high(c):
                        act.wait_ge(w_in[nm][c], 16)
                        nc.scalar.activation(wsplit(WH, c), wraw(c), ACT.Copy).then_inc(S["high_w"], 1)

                    def take(st, key, dst, rows, n, scale=1.0, bias=None):
                        act.wait_ge(S["product"], st.jobs.upto(key))
                        src = PJ[st.jobs.slot(key)][0:rows, 0:n]
                        if bias is None and scale == 1.0:
                            return nc.scalar.activation(dst, src, ACT.Copy)
                        return nc.scalar.activation(dst, src, ACT.Identity, bias=0.0 if bias is None else bias, scale=scale)

                    def to_split(st, key, n, **kw):
                        s = st.splits.upto(key)
                        if not isinstance(s, int) or s > 2:
                            act.wait_ge(S["split"], s - 2)
                        take(st, key, T32[:, st.splits.slot(key), 0:n], 128, n, **kw).then_inc(S["taken"], 1)

                    def context(st, u):
                        for k in range(KE):
                            kw = {"scale": col(nm + "cg", k), "bias": col(nm + "cb", k)} if L.ctx_norm else {}
                            to_split(st, ("ctx", u, k), SK, **kw)

                    def keys(st, u, t0, t1):
                        for t in range(t0, t1):
                            to_split(st, ("K", u, t), SKE, **({} if L.wide else {"bias": col(nm + "bk", t)}))

                    def query_turn(st, u):
                        for k in range(KE):
                            kw = {"scale": col("nw", k)} if nm == "L1" else {} if nm == "L2" else {"scale": col(nm + "xg", k), "bias": col(nm + "xb", k)}
                            to_split(st, ("xT", u, k), 2 * SQ, **kw)

                    def queries(st, u):
                        for t in range(L.nt):
                            to_split(st, ("Q", u, t), 2 * SQ, **({} if L.wide else {"bias": col(nm + "bq", t)}))

                    def values(st, u):
                        for c in range(L.nv):
                            t, part = c % KV_TILES, c // KV_TILES
                            r = KV_ROWS[t]
                            if L.wide:
                                dst = V[0:r, t * L.hw + part * L.vn:t * L.hw + part * L.vn + L.vn]
                                take(st, ("V", u, c), dst, r, L.vn).then_inc(S["taken"], 1)
                            else:
                                act.wait_ge(S["product"], st.jobs.upto(("V", u, c)))
                                dst = V[0:r, t * L.hw:t * L.hw + L.hw].rearrange("p (h d) -> p h d", h=H)[:, :, 0:16]
                                src = PJ[st.jobs.slot(("V", u, c))][0:r, 0:L.vn].rearrange("p (h d) -> p h d", h=H)
                                nc.scalar.activation(dst, src, ACT.Copy).then_inc(S["taken"], 1)

                    def heads(st, u):
                        for s in range(H):
                            act.wait_ge(S["maxed"], st.head(u, s))
                            act.wait_ge(S["turned"], st.head(u, s))
                            nc.scalar.activation(P[:, s % 4, 0:SK], PS_[s % 2][0:SQ, 0:SK], ACT.Exp, bias=MX[:, u, s:s + 1],
                                                 scale=1.0, accum_out=DEN[:, u, s:s + 1]).then_inc(S["exped"], 1)
                            if s == 11 and st.has_next(u):
                                context(st, u)

                    def spread(st, u):
                        for r in range(L.nr):
                            act.wait_ge(S["product"], st.jobs.upto(("R", u, r)))
                            nc.scalar.activation(OT[:, 4 * r:4 * r + 4, :].rearrange("p t q -> p (t q)"),
                                                 PJ[st.jobs.slot(("R", u, r))][:, 0:4 * SQ], ACT.Copy).then_inc(S["taken"], 1)

                    st = Stage(L, -1)
                    split_high(0)
                    context(st, -1)
                    query_turn(st, -1)
                    split_high(1)
                    split_high(2)
                    keys(st, -1, 0, L.nt)
                    queries(st, -1)
                    if not L.wide:
                        act.wait_ge(S["cleared_v"], 1)
                    values(st, -1)

                    def body(st):
                        for u in range(2):
                            heads(st, u)
                            if st.has_pair(u):
                                query_turn(st, u)
                            if st.has_next(u):
                                keys(st, u, 0, L.half)
                            spread(st, u)
                            if st.has_next(u):
                                keys(st, u, L.half, L.nt)
                            if st.has_pair(u):
                                queries(st, u)
                            take(st, ("out", u, 0), Y[:, :], SQ, E).then_inc(S["taken"], 1)
                            if st.has_next(u):
                                values(st, u)
                    loop(act, body)

                @block.vector
                def _(dve):
                    dve.sem_inc(S["unloaded"], 2)
                    dve.sem_inc(S["freed"], L.nr)
                    q_scale = {"L0": 0.25, "L1": 1.0, "L2": 0.125, "L3": 0.25}[nm]

                    def split_low(c):
                        dve.wait_ge(S["high_w"], c + 1)
                        nc.vector.tensor_tensor(wsplit(WL, c), wraw(c), wsplit(WH, c).bitcast(fp32), ALU.subtract).then_inc(S["low_w"], 1)

                    def stats(st, key, rows, srcs, at):
                        m = st.norms.upto(key)
                        for n, (r, src) in enumerate(zip(rows, srcs)):
                            last = nc.vector.bn_stats(BN[0:r, at + n, :], src)
                        last.then_inc(S["stats"], 1)
                        wait_apart(dve, S["stats"], m)
                        for n, r in enumerate(rows):
                            last = nc.vector.bn_aggr(MV[0:r, at + n, :], BN[0:r, at + n, :])
                        last.then_inc(S["moments"], 1)

                    def context_stats(st, u):
                        n = 0 if st.first else 1 - u
                        wait_apart(dve, s_c[n], 32 if st.first else st.i * 32 + 32 * (u + 1))
                        stats(st, ("ctx", u), KV_ROWS, [C[0:r, n, t, :] for t, r in enumerate(KV_ROWS)], 0)

                    def context_norm(st, u):
                        n, m = 0 if st.first else 1 - u, st.norms.upto(("ctx", u))
                        dve.wait_ge(S["rstd"], m)
                        for t, r in enumerate(KV_ROWS):
                            last = nc.vector.tensor_scalar(CN[0:r, t, :], C[0:r, n, t, :], MV[0:r, t, 0:1], RS[0:r, t:t + 1], ALU.subtract, ALU.mult)
                        last.then_inc(S["normed"], 1)

                    def x_rows(st, v):
                        b = v if st.first else st.i * 2 + 2 + v
                        return X[:, b, :]

                    def x_stats(st, u):
                        stats(st, ("x", u), [SQ, SQ], [x_rows(st, v) for v in range(2)], 0)

                    def x_norm(st, u):
                        dve.wait_ge(S["rstd"], st.norms.upto(("x", u)))
                        for v in range(2):
                            if nm == "L1":
                                last = nc.vector.tensor_scalar(XN[:, v, :], x_rows(st, v), RS[0:SQ, v:v + 1], None, ALU.mult)
                            else:
                                last = nc.vector.tensor_scalar(XN[:, v, :], x_rows(st, v), MV[0:SQ, v, 0:1], RS[0:SQ, v:v + 1], ALU.subtract, ALU.mult)
                        last.then_inc(S["normed"], 1)

                    def x_copy(st, u):
                        for v in range(2):
                            last = nc.vector.tensor_copy(XN[:, v, :], x_rows(st, v))
                        last.then_inc(S["copied"], 1)

                    def split(st, key):
                        kind, u, t = key
                        s, j = st.splits.upto(key), st.jobs.upto(key)
                        n = {"ctx": SK, "K": SKE}.get(kind, 2 * SQ)
                        hi, lo = {"ctx": (CTH, CTL), "xT": (XTH, XTL), "K": (KH, KL), "Q": (QH, QL)}[kind]
                        hi, lo = hi[:, t, 0:n], lo[:, t, 0:n]
                        src = T32[:, st.splits.slot(key), 0:n]
                        if L.rope and kind in "KQ":
                            src = AC[:, st.turns.slot(key), 0:n]
                            r = st.turns.upto(key)
                            dve.wait_ge(S["rotated"], r)
                            nc.vector.tensor_tensor(src, src, SH[:, st.turns.slot(key), 0:n], ALU.add).then_inc(S["joined"], 1)
                            dve.wait_ge(S["joined"], r)
                        else:
                            dve.wait_ge(S["taken"], j)
                        scale = q_scale if kind == "Q" else 1.0
                        narrow_key = kind == "K" and not L.wide
                        if narrow_key:
                            hi = KR[:, st.splits.slot(key), 0:n]
                        if scale != 1.0:
                            nc.vector.tensor_scalar(hi, src, scale, None, ALU.mult).then_inc(S["rounded"], 1)
                        else:
                            nc.vector.tensor_copy(hi, src).then_inc(S["rounded"], 1)
                        dve.wait_ge(S["rounded"], s)
                        if narrow_key:
                            nc.vector.scalar_tensor_tensor(out=KH[:, t, :], in0=hi.bitcast(fp32), scalar=low_half, in1=src,
                                                           op0=ALU.mult, op1=ALU.add).then_inc(S["split"], 1)
                        elif scale != 1.0:
                            nc.vector.scalar_tensor_tensor(out=lo, in0=src, scalar=scale, in1=hi.bitcast(fp32),
                                                           op0=ALU.mult, op1=ALU.subtract).then_inc(S["split"], 1)
                        else:
                            nc.vector.tensor_tensor(lo, src, hi.bitcast(fp32), ALU.subtract).then_inc(S["split"], 1)

                    def shuffle(st, key):
                        n = SKE if key[0] == "K" else 2 * SQ
                        wait_apart(dve, S["taken"], st.jobs.upto(key))
                        nc.vector.stream_shuffle(SH[:, st.turns.slot(key), 0:n], T32[:, st.splits.slot(key), 0:n],
                                                 [p ^ 1 for p in range(32)]).then_inc(S["shuffled"], 1)

                    def splits(st, todo):
                        if L.rope and todo[0][0] in "KQ":
                            shuffle(st, todo[0])
                            for this, then in zip(todo, todo[1:] + [None]):
                                if then:
                                    shuffle(st, then)
                                split(st, this)
                        else:
                            for key in todo:
                                split(st, key)

                    def heads(st, u):
                        for s in range(H + 2):
                            if s < H:
                                dve.wait_ge(S["scores"], st.head(u, s))
                                nc.vector.tensor_reduce(MX[:, u, s:s + 1], PS_[s % 2][0:SQ, 0:SK], AX.X, ALU.max,
                                                        negate=True).then_inc(S["maxed"], 1)
                            if s >= 2:
                                h = s - 2
                                dve.wait_ge(S["turned"], st.head(u, h) + 4)
                                dve.wait_ge(S["weighed"], st.head(u, h))
                                nc.vector.tensor_copy(PT[:, h % 2, :], PP[h % 2][:, 0:KV_TILES * SQ]).then_inc(S["unloaded"], 1)
                            if st.has_next(u):
                                if L.ctx_norm and s == 3:
                                    context_stats(st, u)
                                if L.ctx_norm and s == 6:
                                    context_norm(st, u)
                                if s == 13:
                                    splits(st, [("ctx", u, k) for k in range(KE)])
                            if st.has_pair(u):
                                if L.x_norm and s == 8:
                                    x_stats(st, u)
                                if L.x_norm and s == 11:
                                    x_norm(st, u)
                                if not L.x_norm and s == 8:
                                    x_copy(st, u)

                    def invert(st, u):
                        dve.wait_ge(S["exped"], st.head(u, H - 1) + 2)
                        nc.vector.reciprocal(RDEN[:, :], DEN[:, u, :]).then_inc(S["inverse"], 1)
                        dve.wait_ge(S["inverse"], st.batch(u) + 1)
                        nc.vector.tensor_copy(RX[:, 0:L.hw].rearrange("p (h r) -> p h r", h=H),
                                              RDEN[:, :].unsqueeze(2).to_broadcast([SQ, H, L.rows])).then_inc(S["repeated"], 1)

                    def scale(st, u):
                        for r in range(L.nr):
                            dve.wait_ge(S["taken"], st.jobs.upto(("R", u, r)))
                            o = OT[:, 4 * r:4 * r + 4, :].rearrange("p t q -> p (t q)")
                            last = nc.vector.tensor_tensor(o, PO[r][:, 0:4 * SQ], o, ALU.mult).then_inc(S["freed"], 1)
                        dve.wait_ge(S["freed"], (st.batch(u) + 2) * L.nr)
                        if L.wide:
                            dve.sem_inc(S["scaled"], 1)
                        else:
                            for t in range(L.nt):
                                last = nc.vector.tensor_scalar(OT[:, t, :], OT[:, t, :], col(nm + "bv", t), None, ALU.add)
                            last.then_inc(S["scaled"], 1)

                    def finish(st, u):
                        n = st.batch(u)
                        x = X[:, n, :]
                        dve.wait_ge(S["taken"], st.jobs.upto(("out", u, 0)))
                        if nm == "L1":
                            nc.vector.tensor_tensor(x, x, Y[:, :], ALU.add).then_inc(S["summed"], 1)
                            return
                        nc.vector.tensor_tensor(x, x, Y[:, :], ALU.add).then_inc(S["added"], 1)
                        wait_apart(dve, S["added"], n + 1)
                        if nm != "L2":
                            nc.vector.tensor_tensor(x, x, ROWS[:, 0 if nm == "L0" else 4, :], ALU.add).then_inc(S["summed"], 1)
                            return
                        stats(st, ("post", u), [SQ], [x], 3)
                        dve.wait_ge(S["rstd"], st.norms.upto(("post", u)))
                        nc.vector.tensor_scalar(Y[:, :], x, MV[0:SQ, 3, 0:1], RS[0:SQ, 3:4], ALU.subtract, ALU.mult).then_inc(S["normed"], 1)
                        dve.wait_ge(S["normed"], st.norms.upto(("post", u)))
                        nc.vector.tensor_tensor(Y[:, :], Y[:, :], ROWS[:, 2, :], ALU.mult).then_inc(S["gammaed"], 1)
                        dve.wait_ge(S["gammaed"], n + 1)
                        nc.vector.tensor_tensor(x, Y[:, :], ROWS[:, 3, :], ALU.add).then_inc(S["summed"], 1)

                    st = Stage(L, -1)
                    if L.ctx_norm:
                        context_stats(st, -1)
                        context_norm(st, -1)
                    if L.x_norm:
                        x_stats(st, -1)
                        x_norm(st, -1)
                    else:
                        x_copy(st, -1)
                    split_low(0)
                    splits(st, [("ctx", -1, k) for k in range(KE)])
                    splits(st, [("xT", -1, k) for k in range(KE)])
                    split_low(1)
                    split_low(2)
                    splits(st, [("K", -1, t) for t in range(L.nt)])
                    splits(st, [("Q", -1, t) for t in range(L.nt)])

                    def body(st):
                        for u in range(2):
                            heads(st, u)
                            invert(st, u)
                            if st.has_pair(u):
                                splits(st, [("xT", u, k) for k in range(KE)])
                            if st.has_next(u):
                                splits(st, [("K", u, t) for t in range(L.half)])
                            scale(st, u)
                            if st.has_next(u):
                                splits(st, [("K", u, t) for t in range(L.half, L.nt)])
                            if st.has_pair(u):
                                splits(st, [("Q", u, t) for t in range(L.nt)])
                            finish(st, u)
                    loop(dve, body)

                @block.gpsimd
                def _(pool):
                    if not L.wide:
                        nc.gpsimd.memset(WO[:, 0:4 * E], 0.0).then_inc(S["cleared_w"], 1)
                        nc.gpsimd.memset(V[:, 0:KV_TILES * L.hw], 0.0).then_inc(S["cleared_v"], 1)

                    def rstd(st, key, at, n, eps):
                        m = st.norms.upto(key)
                        wait_apart(pool, S["moments"], m)
                        ve, mean, var = VE[:, at:at + n], MV[:, at:at + n, 0], MV[:, at:at + n, 1]
                        if nm == "L1":
                            nc.gpsimd.tensor_tensor(ve, mean, mean, ALU.mult).then_inc(S["square"], 1)
                            pool.wait_ge(S["square"], m)
                            nc.gpsimd.tensor_tensor(SQV[:, at:at + n], ve, var, ALU.add).then_inc(S["squares"], 1)
                            wait_apart(pool, S["squares"], m)
                            var = SQV[:, at:at + n]
                        nc.gpsimd.tensor_scalar(EV[:, at:at + n], var, eps, None, ALU.add).then_inc(S["powers"], 1)
                        pool.wait_ge(S["powers"], m)
                        nc.gpsimd.tensor_tensor(RS[:, at:at + n], EV[:, at:at + n], HALF[:, at:at + n], ALU.pow).then_inc(S["rstd"], 1)

                    def tables(st, u):
                        slot = 0 if st.first else 1 - u
                        n = 1 if st.first else st.batch(u) + 2
                        wait_apart(pool, s_m[slot], 16 if st.first else st.i * 16 + 16 * (u + 1))
                        nc.gpsimd.tensor_copy(MF[:, :], M8[:, slot, :]).then_inc(S["mask_float"], 1)
                        wait_apart(pool, S["mask_float"], n)
                        nc.gpsimd.tensor_tensor(COSM[:, :], cos, MF[:, :], ALU.mult)
                        nc.gpsimd.tensor_tensor(SINM[:, :], sin, MF[:, :], ALU.mult)
                        nc.gpsimd.tensor_scalar(MNEG[:, slot, :], MF[0:2, :], -1.0, None, ALU.add).then_inc(S["mask_tables"], 1)
                        wait_apart(pool, S["mask_tables"], n)

                    def rotate(st, todo):
                        for key in todo:
                            r, slot, keys = st.turns.upto(key), st.turns.slot(key), key[0] == "K"
                            src = T32[:, st.splits.slot(key), 0:SKE if keys else 2 * SQ]
                            ac, sh, c, s = AC[:, slot, :], SH[:, slot, :], COSM[:, :], SINM[:, :]
                            if not keys:
                                src, ac, sh = [x[:, 0:2 * SQ].rearrange("p (v q) -> p v q", v=2) for x in (src, ac, sh)]
                                c, s = [x[:, 0:SQ].unsqueeze(1).to_broadcast([128, 2, SQ]) for x in (cos, sin)]
                            pool.wait_ge(S["shuffled"], r)
                            nc.gpsimd.tensor_tensor(ac, src, c, ALU.mult)
                            nc.gpsimd.tensor_tensor(sh, sh, s, ALU.mult).then_inc(S["rotated"], 1)

                    def segment(st, u):
                        if L.rope and st.has_next(u):
                            tables(st, u)
                        if L.ctx_norm and st.has_next(u):
                            rstd(st, ("ctx", u), 0, KV_TILES, L.eps)
                        if L.x_norm and st.has_pair(u):
                            rstd(st, ("x", u), 0, 2, L.eps)
                        if L.rope and st.has_next(u):
                            rotate(st, [("K", u, t) for t in range(L.nt)])
                        if L.rope and st.has_pair(u):
                            rotate(st, [("Q", u, t) for t in range(L.nt)])
                        if L.eps_post is not None and not st.first:
                            rstd(st, ("post", u), 3, 1, L.eps_post)

                    segment(Stage(L, -1), -1)

                    def body(st):
                        for u in range(2):
                            segment(st, u)
                    loop(pool, body)

        def feed_forward():
            G = 4
            nf = FF // 128
            per = KE + nf + G
            YN = RX[:, :].rearrange("p (g e) -> p g e", g=G)
            YH, YL = [K_[:, :, :].rearrange("p t n -> p (t n)")[:, 0:KE * G * SQ].rearrange("p (k n) -> p k n", k=KE) for K_ in (KH, KL)]
            HT = V[:, 0:nf * G * SQ].rearrange("p (t n) -> p t n", t=nf)
            FB = PJ
            assert per % 2 == 0
            nb = len(FB)
            TB = [FB[k] for k in range(KE)]
            with nc.Block() as block:

                @block.sync
                def _(sp):
                    load_output_weights(sp, "ffn")
                    sp.wait_ge(S["low_w"], 1)
                    load_weights(sp, "L1")

                @block.tensor
                def _(pe):
                    pe.sem_inc(S["taken"], nb)
                    with pe.Fori(0, B // G) as i:
                        pe.wait_ge(S["normed"], i + 1)
                        for k in range(KE):
                            pe.wait_ge(S["taken"], i * per + (k + 1))
                            for g in range(G):
                                last = nc.tensor.transpose(TB[k][:, SQ * g:SQ * g + SQ], YN[:, g, 128 * k:128 * k + 128], ident[0:SQ, 0:SQ])
                            last.then_inc(S["product"], 1)
                        pe.wait_ge(S["low_w"], 1)
                        pe.wait_ge(S["split"], (i + 1) * KE)
                        for t in range(nf):
                            n = KE + t
                            pe.wait_ge(S["taken"], i * per + (n + 1))
                            todo = [x for k in range(KE) for lh, ll in [[W[:, FF * k + 128 * t:FF * k + 128 * t + 128] for W in (WH, WL)]]
                                    for x in ((lh, YH[:, k, :]), (lh, YL[:, k, :]), (ll, YH[:, k, :]))]
                            for m, (x, y) in enumerate(todo):
                                last = nc.tensor.matmul(FB[n % nb][:, 0:G * SQ], x, y, start=m == 0, stop=m == len(todo) - 1)
                            last.then_inc(S["product"], 1)
                        pe.wait_ge(wo_in["ffn"], 16)
                        pe.wait_ge(S["taken"], i * per + (KE + nf + nb))
                        for g in range(G):
                            n = KE + nf + g
                            pe.wait_ge(S["taken"], i * per + (n + 1))
                            for t in range(nf):
                                last = nc.tensor.matmul(FB[n % nb][0:SQ, 0:E], HT[:, t, SQ * g:SQ * g + SQ], WO[:, E * t:E * t + E],
                                                        start=t == 0, stop=t == nf - 1)
                            last.then_inc(S["product"], 1)

                @block.scalar
                def _(act):
                    act.wait_ge(w_in["ffn"][0], 16)
                    nc.scalar.activation(WH[:, 0:KE * FF], W_RAW[:, 0, :], ACT.Copy).then_inc(S["high_w"], 1)
                    with act.Fori(0, B // G) as i:
                        for k in range(KE):
                            act.wait_ge(S["product"], i * per + (k + 1))
                            nc.scalar.activation(T32[:, k, :], TB[k][:, 0:G * SQ], ACT.Identity, bias=col("b2n", k),
                                                 scale=col("g2", k)).then_inc(S["taken"], 1)
                        for t in range(nf):
                            act.wait_ge(S["product"], i * per + (KE + t + 1))
                            nc.scalar.activation(HT[:, t, :], FB[(KE + t) % nb][:, 0:G * SQ], ACT.Gelu, bias=col("b1", t)).then_inc(S["taken"], 1)
                        for g in range(G):
                            n = KE + nf + g
                            act.wait_ge(S["product"], i * per + (n + 1))
                            nc.scalar.activation(P[:, g, 0:E], FB[n % nb][0:SQ, 0:E], ACT.Copy).then_inc(S["taken"], 1)

                @block.vector
                def _(dve):
                    dve.wait_ge(S["high_w"], 1)
                    nc.vector.tensor_tensor(WL[:, 0:KE * FF], W_RAW[:, 0, :], WH[:, 0:KE * FF].bitcast(fp32), ALU.subtract).then_inc(S["low_w"], 1)
                    with dve.Fori(0, B // G) as i:
                        for g in range(G):
                            last = nc.vector.bn_stats(BN[0:SQ, g, :], X[:, i * G + g, :])
                        last.then_inc(S["stats"], 1)
                        wait_apart(dve, S["stats"], i + 1)
                        for g in range(G):
                            last = nc.vector.bn_aggr(MV[0:SQ, g, :], BN[0:SQ, g, :])
                        last.then_inc(S["moments"], 1)
                        dve.wait_ge(S["rstd"], i + 1)
                        for g in range(G):
                            last = nc.vector.tensor_scalar(YN[:, g, :], X[:, i * G + g, :], MV[0:SQ, g, 0:1], RS[0:SQ, g:g + 1], ALU.subtract, ALU.mult)
                        last.then_inc(S["normed"], 1)
                        for k in range(KE):
                            dve.wait_ge(S["taken"], i * per + (k + 1 + nb))
                            nc.vector.tensor_copy(YH[:, k, :], T32[:, k, :]).then_inc(S["rounded"], 1)
                            dve.wait_ge(S["rounded"], i * KE + (k + 1))
                            nc.vector.tensor_tensor(YL[:, k, :], T32[:, k, :], YH[:, k, :].bitcast(fp32), ALU.subtract).then_inc(S["split"], 1)
                        for g in range(G):
                            x = X[:, i * G + g, :]
                            dve.wait_ge(S["taken"], i * per + (KE + nf + g + 1 + nb))
                            nc.vector.tensor_tensor(x, x, P[:, g, 0:E], ALU.add).then_inc(S["added"], 1)
                            dve.wait_ge(S["added"], i * G + (g + 1))
                            nc.vector.tensor_tensor(x, x, ROWS[:, 1, :], ALU.add).then_inc(S["summed"], 1)

                @block.gpsimd
                def _(pool):
                    with pool.Fori(0, B // G) as i:
                        wait_apart(pool, S["moments"], i + 1)
                        nc.gpsimd.tensor_scalar(EV[:, :], MV[:, :, 1], 1e-5, None, ALU.add).then_inc(S["powers"], 1)
                        pool.wait_ge(S["powers"], i + 1)
                        nc.gpsimd.tensor_tensor(RS[:, :], EV[:, :], HALF[:, :], ALU.pow).then_inc(S["rstd"], 1)

        for ph, what in enumerate(PHASES):
            if ph:
                clear_semaphores()
            if what == "ffn":
                feed_forward()
            else:
                attention(what, ph)


def constants():
    import numpy as np
    c = np.zeros((128, C_END), np.float32)
    c[:, C_ID:C_ID + 128] = np.eye(128)
    d = np.arange(128) % 64
    inv = (1.0 / np.float32(10000.0) ** (((d // 2) * 2).astype(np.float32) / np.float32(64))).astype(np.float32)
    ang = (np.arange(SKE, dtype=np.float32)[None, :] * inv[:, None]).astype(np.float32).astype(np.float64)
    c[:, C_COS:C_COS + SKE] = np.cos(ang)
    c[:, C_SIN:C_SIN + SKE] = np.sin(ang) * np.where(d % 2 == 0, -1.0, 1.0)[:, None]
    c[:, C_NEG] = np.where(np.arange(128) % 32 >= 16, -1.0, 0.0)
    high = float(int(NEG) >> 18 << 18)
    c[0, C_FILL:C_FILL + SQ], c[1, C_FILL:C_FILL + SQ] = high, NEG - high
    return c


def vectors(a):
    import numpy as np
    out = np.zeros((128, VEC_END), np.float32)

    def tiles(name, src):
        v = np.asarray(a[src]).reshape(-1, 128)
        for k in range(v.shape[0]):
            out[:, VEC_COLS[name] + k] = v[k]
    for p, names in (("L0", ("ln1_g", "ln1_b", "ln1_g", "ln1_b")), ("L3", ("gkv", "betakv", "gq", "betaq"))):
        for v, src in zip(("cg", "cb", "xg", "xb"), names):
            tiles(p + v, f"{p}_xattn_{src}")
        for v in ("bq", "bk", "bv"):
            h = np.asarray(a[f"{p}_xattn_{v}"]).reshape(4, 4, 16)
            for t in range(4):
                for g in range(4):
                    for twice in range(1 if v == "bv" else 2):
                        r = 32 * g + 16 * twice
                        out[r:r + 16, VEC_COLS[p + v] + t] = h[t, g]
    for v, src in (("g2", "L0_xattn_ln2_g"), ("b2n", "L0_xattn_ln2_b"), ("b1", "L0_xattn_b1"), ("nw", "L1_xattn_norm_w")):
        tiles(v, src)
    return out


def kernel(**inputs):
    import numpy as np
    import concourse.bacc as bacc
    from concourse.bass_utils import run_bass_kernel_spmd

    nc = bacc.Bacc("TRN2", target_bir_lowering=False, num_devices=1)
    arrays, args = {}, {}
    for name, value in inputs.items():
        v = np.ascontiguousarray(value)
        short = "mask" if name == "mask_BxS2_bf1" else name
        if short == "mask":
            v = v.view(np.uint8)
        arrays[f"in_{short}"] = v
        args[short] = nc.dram_tensor(f"in_{short}", v.shape, mybir.dt.from_np(v.dtype), kind="ExternalInput").ap()
    arrays["vectors"] = vectors(inputs)
    args["vectors"] = nc.dram_tensor("vectors", (128, VEC_END), fp32, kind="ExternalInput").ap()
    arrays["constants"] = constants()
    consts = nc.dram_tensor("constants", (128, C_END), fp32, kind="ExternalInput").ap()
    out = nc.dram_tensor("out", (B, SQ, E), fp32, kind="ExternalOutput").ap()
    build(nc, args, consts, out)
    r = run_bass_kernel_spmd(nc, [{**arrays}], core_ids=[0])
    return r.results[0]["out"]
```

```python
import concourse.bass as bass
from concourse import mybir
from contextlib import ExitStack

fp32 = mybir.dt.float32
f32r = mybir.dt.float32r
u8 = mybir.dt.uint8
ALU = mybir.AluOpType
ACT = mybir.ActivationFunctionType
AX = mybir.AxisListType

B, SQ, SK, E, H = 16, 100, 361, 256, 16
KE = E // 128
KV_TILES = -(-SK // 128)
KV_ROWS = [min(128, SK - 128 * t) for t in range(KV_TILES)]
SKP = 128 * KV_TILES
SKE = SK + SK % 2
PAIRS = B // 2
FF = 4 * E
NEG = 1.0e9

C_ID, C_COS, C_SIN, C_NEG = 0, 128, 128 + SKE, 128 + 2 * SKE
C_FILL, C_OWN = C_NEG + 1, C_NEG + 1 + SQ
C_END = C_OWN + 4


VEC_COLS, VEC_END = {}, 0
for _p in ("L0", "L3"):
    for _v, _n in (("cg", KE), ("cb", KE), ("xg", KE), ("xb", KE), ("bq", 4), ("bk", 4), ("bv", 4)):
        VEC_COLS[_p + _v], VEC_END = VEC_END, VEC_END + _n
for _v, _n in (("g2", KE), ("b2n", KE), ("b1", FF // 128), ("nw", KE)):
    VEC_COLS[_v], VEC_END = VEC_END, VEC_END + _n


class Layer:

    def __init__(self, name, hd, ctx_norm, x_norm, rope, eps, eps_post=None):
        self.name, self.hd, self.ctx_norm, self.x_norm, self.rope = name, hd, ctx_norm, x_norm, rope
        self.eps, self.eps_post = eps, eps_post
        self.wide = hd == 64
        self.rows = 64 if self.wide else 32
        self.per = 128 // self.rows
        self.nt = H // self.per
        self.hw = self.rows * H
        self.vn = 512 if self.wide else 256
        self.nv = KV_TILES * (hd * H // self.vn)
        self.nr = -(-self.nt // 4)
        self.half = self.nt // 2


class Steps:

    def __init__(self, keys, base, parity=0):
        self.at = {k: n for n, k in enumerate(keys)}
        assert len(self.at) == len(keys)
        self.base, self.parity, self.count = base, parity, len(keys)

    def upto(self, key):
        return self.base + (self.at[key] + 1)

    def slot(self, key):
        return (self.parity + self.at[key]) % 2

    def before(self, u):
        return self.base + sum(1 for k in self.at if k[1] < u)


class Stage:

    def __init__(self, L, i, last=False):
        self.i, self.last, self.first = i, last, isinstance(i, int) and i < 0
        self.L = L
        jobs0 = self.jobs_of(L, -1, False)
        jobs1 = self.jobs_of(L, 0, False)
        splits0, splits1 = [[k for k in j if k[0] in ("ctx", "K", "xT", "Q")] for j in (jobs0, jobs1)]
        norms0, norms1 = self.norms_of(L, -1, False), self.norms_of(L, 0, False)
        assert len(jobs1) % 2 == 0 and len(splits1) % 2 == 0
        jobs = self.jobs_of(L, -1 if self.first else 0, last)
        splits = [k for k in jobs if k[0] in ("ctx", "K", "xT", "Q")]
        norms = self.norms_of(L, -1 if self.first else 0, last)

        def base(a, b):
            return 0 if self.first else len(a) + i * len(b)
        self.jobs = Steps(jobs, base(jobs0, jobs1), 0 if self.first else len(jobs0) % 2)
        self.splits = Steps(splits, base(splits0, splits1), 0 if self.first else len(splits0) % 2)
        self.norms = Steps(norms, base(norms0, norms1))
        turns0, turns1, turns = [[k for k in j if k[0] in "KQ"] for j in (jobs0, jobs1, jobs)]
        assert len(turns1) % 2 == 0
        self.turns = Steps(turns, base(turns0, turns1), 0 if self.first else len(turns0) % 2)

    def has_next(self, u):
        return not (self.last and u == 1)

    def has_after(self, u):
        return not self.last

    def has_pair(self, u):
        return self.first or (u == 1 and not self.last)

    def keys_split(self, u):
        if u == 0:
            return self.splits.base
        return self.splits.upto(("K", 0, self.L.nt - 1))

    def values_taken(self, u):
        return self.jobs.base if u == 0 else self.jobs.upto(("V", 0, self.L.nv - 1))

    def context_split(self, u):
        return self.splits.before(u)

    @staticmethod
    def jobs_of(L, i, last):
        if i < 0:
            return ([("ctx", -2, k) for k in range(KE)] + [("xT", -1, k) for k in range(KE)]
                    + [("K", -1, t) for t in range(L.nt)] + [("Q", -1, t) for t in range(L.nt)]
                    + [("V", -1, c) for c in range(L.nv)] + [("ctx", -1, k) for k in range(KE)])
        out = []
        for u in range(2):
            nxt, pair = not (last and u == 1), u == 1 and not last
            if nxt:
                out += [("K", u, t) for t in range(L.nt)]
            if pair:
                out += [("xT", u, k) for k in range(KE)]
            if nxt:
                out += [("V", u, c) for c in range(L.nv - 2)]
            out += [("R", u, r) for r in range(L.nr)]
            if nxt:
                out += [("V", u, c) for c in range(L.nv - 2, L.nv)]
            if not last:
                out += [("ctx", u, k) for k in range(KE)]
            if pair:
                out += [("Q", u, t) for t in range(L.nt)]
            out.append(("out", u, 0))
        return out

    @staticmethod
    def norms_of(L, i, last):
        if i < 0:
            return ([("ctx", -2)] if L.ctx_norm else []) + ([("x", -1)] if L.x_norm else []) + ([("ctx", -1)] if L.ctx_norm else [])
        out = []
        for u in range(2):
            if L.ctx_norm and not last:
                out.append(("ctx", u))
            if L.x_norm and u == 1 and not last:
                out.append(("x", u))
            if L.eps_post is not None:
                out.append(("post", u))
        return out

    def pair(self):
        return 1 if self.first else self.i + 2

    def batch(self, u):
        return self.i * 2 + u

    def own(self, u, t):
        return self.i * 8 + (4 * u + t + 1)

    def half_head(self, u, h):
        return self.i * H + (H // 2 * u + h // 2 + 1)

    def of_three(self, u, h):
        return self.head(u, max(h, 2)) - 1

    def head(self, u, h):
        return self.i * (2 * H) + (H * u + h + 1)


PASSED = []


def wait_apart(eng, s, value):
    eng.wait_ge(s, value)
    eng.sem_inc(PASSED[0], 1)


def build(nc, a, consts, out):
    stack = ExitStack()
    with stack:
        def sb(name, shape, dt=fp32):
            return stack.enter_context(nc.sbuf_tensor(name, shape, dt))

        def ps(name, shape):
            return stack.enter_context(nc.psum_tensor(name, shape, fp32))

        def sem(name):
            return stack.enter_context(nc.semaphore(name))

        X = sb("X", [SQ, B, E])
        CON = sb("CON", [128, C_END])
        ident = CON[:, C_ID:C_ID + 128]
        cos, sin = CON[:, C_COS:C_COS + SKE], CON[:, C_SIN:C_SIN + SKE]
        low_half = CON[:, C_NEG:C_NEG + 1]
        own = CON[:, C_OWN:C_OWN + 4]
        VEC = sb("VEC", [128, VEC_END])
        ROWS = sb("ROWS", [SQ, 5, E])
        W_RAW = sb("W_RAW", [128, 3, 2048])
        WH = sb("WH", [128, 6144], f32r)
        WL = sb("WL", [128, 6144], f32r)
        WO = sb("WO", [128, 2048])
        C = sb("C", [128, 2, KV_TILES, E])
        CTH, CTL = sb("CTH", [128, KE, SKE], f32r), sb("CTL", [128, KE, SKE], f32r)
        KH, KL = sb("KH", [128, 8, SKE], f32r), sb("KL", [128, 8, SKE], f32r)
        KR = KL[:, 0:2, :]
        V = sb("V", [128, 3200])
        QH, QL = sb("QH", [128, 8, 2 * SQ], f32r), sb("QL", [128, 8, 2 * SQ], f32r)
        T32 = sb("T32", [128, 2, 4 * SQ])
        WORK = sb("WORK", [128, 7 * SKE])
        CN = WORK[:, 0:KV_TILES * E].rearrange("p (t e) -> p t e", e=E)
        SH, AC = [WORK[:, n * SKE:(n + 2) * SKE].rearrange("p (s n) -> p s n", s=2) for n in (0, 2)]
        COSM, SINM, MF = [WORK[:, n * SKE:(n + 1) * SKE] for n in (4, 5, 6)]
        M8 = sb("M8", [128, 2, SKE], u8)
        MNEG = sb("MNEG", [2, 2, SKE], f32r)
        FILL = sb("FILL", [2, SQ], f32r)
        XN = sb("XN", [SQ, 2, E])
        XTH, XTL = sb("XTH", [128, KE, 2 * SQ], f32r), sb("XTL", [128, KE, 2 * SQ], f32r)
        P = sb("P", [SQ, 4, SKP])
        PT = sb("PT", [128, 3, KV_TILES * SQ])
        RX = sb("RX", [SQ, H * 64])
        OT = sb("OT", [128, 8, SQ])
        Y = sb("Y", [SQ, E])
        MX = sb("MX", [SQ, 2, H])
        DEN = sb("DEN", [SQ, 2, H])
        RDEN = sb("RDEN", [SQ, H])
        BN = sb("BN", [128, 6, 6])
        MV = sb("MV", [128, 6, 2])
        VE = sb("VE", [128, 6])
        EV = sb("EV", [128, 6])
        SQV = sb("SQV", [128, 6])
        RS = sb("RS", [128, 6])
        HALF = sb("HALF", [128, 6])

        PJ = [ps(f"PJ{n}", [128, 512]) for n in range(2)]
        PS_ = [ps(f"PS{n}", [128, 512]) for n in range(2)]
        PP = [ps(f"PP{n}", [128, 512]) for n in range(2)]
        PO = [ps(f"PO{n}", [128, 512]) for n in range(2)]

        def col(name, k=0):
            c = VEC_COLS[name] + k
            return VEC[:, c:c + 1]

        LAYERS = [Layer("L0", 16, True, True, False, 1e-5), Layer("L1", 64, False, True, False, 1e-6),
                  Layer("L2", 64, False, False, True, None, 1e-3), Layer("L3", 16, True, True, False, 1e-5)]
        PHASES = [LAYERS[0], "ffn", LAYERS[1], LAYERS[2], LAYERS[3]]
        names = ["L0", "ffn", "L1", "L2", "L3"]
        w_in = {n: [sem(f"{n}_w{c}_in") for c in range(3)] for n in names}
        wo_in = {n: sem(f"{n}_wo_in") for n in names}
        wo_parts = {"L0": 64, "ffn": 16, "L1": 16, "L2": 16, "L3": 64}

        def raw(c, n):
            return W_RAW[:, c, 0:KE * n].rearrange("p (k n) -> p k n", k=KE)

        def load_weights(eng, n):
            if n == "ffn":
                eng.dma_start(raw(0, FF), a["L0_xattn_w1"].rearrange("(k p) n -> p k n", p=128)).then_inc(w_in[n][0], 16)
                return
            up = {"L0": "L0_xattn_w", "L1": "L1_xattn_w", "L2": "L2_xattn_W", "L3": "L3_xattn_W"}[n]
            width = 1024 if n in ("L1", "L2") else E
            for c, which in enumerate("kvq"):
                eng.dma_start(raw(c, width), a[up + which].rearrange("(k p) n -> p k n", p=128)).then_inc(w_in[n][c], 16)

        def load_output_weights(eng, n):
            if n == "ffn":
                src = a["L0_xattn_w2"]
            elif n in ("L1", "L2"):
                src = a["L1_xattn_wo" if n == "L1" else "L2_xattn_Wo"]
            else:
                src = a[n + ("_xattn_wo" if n == "L0" else "_xattn_Wo")].rearrange("(t g p) n -> g p t n", g=4, p=16)
                for g in range(4):
                    eng.dma_start(WO[32 * g:32 * g + 16, 0:4 * E].rearrange("p (t n) -> p t n", t=4),
                                  src[g]).then_inc(wo_in[n], 16)
                return
            eng.dma_start(WO[:, :].rearrange("p (t n) -> p t n", t=8),
                          src.rearrange("(t p) n -> p t n", p=128)).then_inc(wo_in[n], 16)

        def load_context(eng, n, slot, s_in):
            eng.dma_start(C[:, slot, 0:2, :], a["ctx_1024"][n, 0:256, :].rearrange("(t p) f -> p t f", p=128)).then_inc(s_in[slot], 16)
            eng.dma_start(C[0:KV_ROWS[2], slot, 2, :], a["ctx_1024"][n, 256:SK, :]).then_inc(s_in[slot], 16)

        s_con, s_x, s_vec, s_rows = sem("con_in"), sem("x_in"), sem("vectors_in"), sem("rows_in")
        with nc.Block() as block:
            row_src = ["L0_xattn_bo", "L0_xattn_b2", "L2_xattn_ln_gamma", "L2_xattn_ln_beta", "L3_xattn_bo"]

            @block.sync
            def _(eng):
                load_weights(eng, "L0")
                eng.dma_start(X[:, :, :], a["x"].rearrange("b s f -> s b f")).then_inc(s_x, 16)
                for r, src in enumerate(row_src):
                    eng.dma_start(ROWS[:, r, :], a[src].rearrange("(o n) -> o n", o=1).broadcast_to([SQ, E])).then_inc(s_rows, 16)
                eng.wait_ge(s_rows, 16 * len(row_src))
                eng.wait_ge(s_x, 16)

            @block.scalar
            def _(eng):
                eng.dma_start(CON[:, :], consts).then_inc(s_con, 16)
                eng.dma_start(VEC[:, :], a["vectors"]).then_inc(s_vec, 16)
                eng.wait_ge(s_vec, 16)
                eng.wait_ge(s_con, 16)

            @block.vector
            def _(eng):
                eng.memset(HALF[:, :], -0.5)
                eng.memset(MV[:, :, :], 1.0)
                eng.memset(M8[:, :, SK:SKE], 0)
                for half in (CTH, CTL):
                    eng.memset(half[:, :, SK:SKE].bitcast(fp32), 0.0)
                eng.memset(P[:, :, SK:SKP], 0.0)
                eng.wait_ge(s_con, 16)
                eng.tensor_copy(FILL[:, :], CON[0:2, C_FILL:C_FILL + SQ])

        PASSED[:] = [sem("passed")]
        S = {k: sem(k) for k in
                 ("high_w", "low_w", "cleared_v", "cleared_w",
                  "product",
                  "taken",
                  "rounded",
                  "split",
                  "masked",
                  "scores", "maxed", "exped",
                  "turned", "unloaded_even", "unloaded_odd", "weighed",
                  "inverse", "repeated",
                  "scaled", "freed", "added", "summed",
                  "stats", "moments", "square", "squares", "powers", "rstd", "normed",
                  "copied", "shuffled", "rotated", "joined", "mask_float", "mask_tables", "gammaed")}
        s_c = [sem(f"context{n}_in") for n in range(2)]
        s_m = [sem(f"mask{n}_in") for n in range(2)]
        s_out = sem("out_written")

        def clear_semaphores():
            with nc.Block() as block:

                @block.sync
                def _(sp):
                    for s in [*S.values(), *s_c, *s_m, *PASSED]:
                        sp.sem_clear(s)

        TL, UA, UD, PL = 2, 2, 2, 4
        unloaded = ("unloaded_even", "unloaded_odd")

        def attention(L, ph):
            nm = L.name
            n_ = KE * L.hw
            wk, wv, wq = 0, n_, n_ + KE * L.hd * H
            vw = L.hd * H
            alone = KE * (2 * L.hw + L.hd * H)
            QA = None if L.wide else [W[:, alone:alone + 2 * H * SQ].rearrange("p (v h q) -> p v h q", v=2, h=H) for W in (WH, WL)]

            def scores_of(h):
                return PS_[h % 2] if L.wide else [*PS_, PO[1]][h % 3]

            def wcols(c):
                at, w = ((wk, L.hw), (wv, vw), (wq, L.hw))[c]
                return at, w

            def wsplit(W, c):
                at, w = wcols(c)
                ap = W[:, at:at + KE * w]
                if L.wide or c == 1:
                    return ap
                return ap.rearrange("p (m d e) -> p m d e", d=2, e=16)

            def wraw(c):
                ap = W_RAW[:, c, 0:KE * vw]
                if L.wide or c == 1:
                    return ap
                return ap.rearrange("p (m e) -> p m e", e=16).unsqueeze(2).to_broadcast([128, KE * H, 2, 16])

            def w(W, c, k, n0, n1):
                at, width = wcols(c)
                return W[:, at + k * width + n0:at + k * width + n1]

            def loop(eng, body):
                with eng.Fori(0, PAIRS - 1) as i:
                    body(Stage(L, i))
                body(Stage(L, PAIRS - 1, last=True))

            with nc.Block() as block:

                @block.sync
                def _(sp):
                    for n in range(2):
                        load_context(sp, n, n, s_c)
                        if L.rope:
                            sp.dma_start(M8[:, n, 0:SK], a["mask"][n:n + 1, :].broadcast_to([128, SK])).then_inc(s_m[n], 16)
                    if not L.wide:
                        sp.wait_ge(S["cleared_w"], 1)
                    load_output_weights(sp, nm)
                    if ph < 4:
                        sp.wait_ge(S["low_w"], 3)
                        load_weights(sp, names[ph + 1])

                    def body(st):
                        for u in range(2):
                            if st.last:
                                continue
                            wait_apart(sp, S["scores"], st.head(u, 0))
                            load_context(sp, st.batch(u) + 2, u, s_c)
                            if L.rope:
                                wait_apart(sp, S["mask_tables"], st.batch(u) + 1)
                                n = st.batch(u) + 2
                                sp.dma_start(M8[:, u, 0:SK], a["mask"][bass.ds(n, 1), :].broadcast_to([128, SK])).then_inc(s_m[u], 16)
                    loop(sp, body)
                    if ph == 4:
                        sp.wait_ge(S["summed"], B)
                        sp.dma_start(out.rearrange("b s f -> s b f"), X[:, :, :]).then_inc(s_out, 16)
                        sp.wait_ge(s_out, 16)

                @block.tensor
                def _(pe):
                    pe.sem_inc(S["turned"], 4)
                    pe.sem_inc(S["weighed"], 2)

                    def begin(st, key):
                        j = st.jobs.upto(key)
                        if not isinstance(j, int) or j > 2:
                            pe.wait_ge(S["taken"], j - 2)
                        return PJ[st.jobs.slot(key)]

                    def product3(dst, pairs):
                        todo = [x for lh, ll, rh, rl in pairs for x in ((lh, rh), (lh, rl), (ll, rh))]
                        for n, (l, r) in enumerate(todo):
                            last = nc.tensor.matmul(dst, l, r, start=n == 0, stop=n == len(todo) - 1)
                        return last

                    def context_turn(st, u, n):
                        if L.ctx_norm:
                            pe.wait_ge(S["normed"], st.norms.upto(("ctx", u)))
                        else:
                            pe.wait_ge(s_c[n], 32 if st.first else st.i * 32 + 64)
                        src = CN if L.ctx_norm else C[:, n]
                        for k in range(KE):
                            bank = begin(st, ("ctx", u, k))
                            for t, r in enumerate(KV_ROWS):
                                last = nc.tensor.transpose(bank[:, 128 * t:128 * t + r], src[0:r, t, 128 * k:128 * k + 128], ident[0:r, 0:r])
                            last.then_inc(S["product"], 1)

                    def keys(st, u, todo):
                        if todo[0] == 0:
                            pe.wait_ge(S["split"], st.splits.upto(("ctx", -2, KE - 1)) if st.first else st.context_split(u))
                        for t in todo:
                            bank = begin(st, ("K", u, t))
                            product3(bank[:, 0:SKE], [(w(WH, 0, k, 128 * t, 128 * t + 128), w(WL, 0, k, 128 * t, 128 * t + 128),
                                                      CTH[:, k, :], CTL[:, k, :]) for k in range(KE)]).then_inc(S["product"], 1)

                    def values(st, u, todo):
                        for c in todo:
                            t, part = c % KV_TILES, c // KV_TILES
                            r = KV_ROWS[t]
                            bank = begin(st, ("V", u, c))
                            product3(bank[0:r, 0:L.vn],
                                     [(CTH[:, k, 128 * t:128 * t + r], CTL[:, k, 128 * t:128 * t + r],
                                       w(WH, 1, k, L.vn * part, L.vn * part + L.vn), w(WL, 1, k, L.vn * part, L.vn * part + L.vn))
                                      for k in range(KE)]).then_inc(S["product"], 1)

                    def query_turn(st, u):
                        if L.x_norm:
                            pe.wait_ge(S["normed"], st.norms.upto(("x", u)))
                        else:
                            pe.wait_ge(S["copied"], st.pair())
                        for k in range(KE):
                            bank = begin(st, ("xT", u, k))
                            for v in range(2):
                                last = nc.tensor.transpose(bank[:, SQ * v:SQ * v + SQ], XN[:, v, 128 * k:128 * k + 128], ident[0:SQ, 0:SQ])
                            last.then_inc(S["product"], 1)

                    def queries(st, u):
                        pe.wait_ge(S["split"], st.splits.upto(("xT", u, KE - 1)))
                        for t in range(L.nt):
                            bank = begin(st, ("Q", u, t))
                            product3(bank[:, 0:2 * SQ], [(w(WH, 2, k, 128 * t, 128 * t + 128), w(WL, 2, k, 128 * t, 128 * t + 128),
                                                          XTH[:, k, :], XTL[:, k, :]) for k in range(KE)]).then_inc(S["product"], 1)

                    def heads(st, u):
                        pe.wait_ge(S["split"], st.keys_split(u))
                        if L.rope:
                            pe.wait_ge(S["mask_tables"], st.batch(u) + 1)
                        for s in range(H + PL):
                            if s < H:
                                h, t, r0 = s, s // L.per, L.rows * (s % L.per)
                                pe.wait_ge(S["exped"], st.head(u, h) if L.wide else st.of_three(u, h))
                                q = slice(SQ * u, SQ * u + SQ)
                                qh, ql = QH[r0:r0 + L.rows, t, q], QL[r0:r0 + L.rows, t, q]
                                kh, kl = KH[r0:r0 + L.rows, t, :], KL[r0:r0 + L.rows, t, :]
                                todo = [(qh, kh), (qh, kl), (ql, kh)]
                                if not L.wide:
                                    if s % L.per == 0:
                                        pe.wait_ge(S["masked"], st.own(u, t))
                                    todo = [(Q_[:, u, h, :], KH[:, t, :]) for Q_ in QA]
                                if L.rope:
                                    todo = [(FILL[:, :], MNEG[:, u, :])] + todo
                                for n, (x, y) in enumerate(todo):
                                    last = nc.tensor.matmul(scores_of(h)[0:SQ, 0:SKE], x, y, start=n == 0, stop=n == len(todo) - 1)
                                last.then_inc(S["scores"], 1)
                            if TL <= s < H + TL:
                                h = s - TL
                                pe.wait_ge(S["exped"], st.head(u, h) + 2)
                                pe.wait_ge(S[unloaded[h % 2]], st.half_head(u, h))
                                for t in range(KV_TILES):
                                    last = nc.tensor.transpose(PP[h % 2][:, SQ * t:SQ * t + SQ], P[:, h % 4, 128 * t:128 * t + 128], ident[0:SQ, 0:SQ])
                                last.then_inc(S["turned"], 1)
                            if s >= PL:
                                h = s - PL
                                t, r0 = h // L.per, L.rows * (h % L.per)
                                if h == 0:
                                    pe.wait_ge(S["taken"], st.values_taken(u))
                                    pe.wait_ge(S["freed"], (st.batch(u) + 1) * L.nr)
                                pe.wait_ge(S[unloaded[h % 2]], st.half_head(u, h) + 1)
                                for c, r in enumerate(KV_ROWS):
                                    last = nc.tensor.matmul(PO[t // 4][r0:r0 + L.rows, SQ * (t % 4):SQ * (t % 4) + SQ],
                                                            V[0:r, c * L.hw + L.rows * h:c * L.hw + L.rows * h + L.rows],
                                                            PT[0:r, h % 3, SQ * c:SQ * c + SQ], start=c == 0, stop=c == KV_TILES - 1)
                                last.then_inc(S["weighed"], 1)
                            if st.has_next(u) and 0 < s <= H and s % L.per == 0:
                                keys(st, u, [s // L.per - 1])

                    def spread(st, u):
                        pe.wait_ge(S["repeated"], st.batch(u) + 1)
                        for r in range(L.nr):
                            bank = begin(st, ("R", u, r))
                            for t in range(4):
                                c = 128 * (4 * r + t)
                                last = nc.tensor.transpose(bank[:, SQ * t:SQ * t + SQ], RX[:, c:c + 128], ident[0:SQ, 0:SQ])
                            last.then_inc(S["product"], 1)

                    def project(st, u):
                        bank = begin(st, ("out", u, 0))
                        pe.wait_ge(S["scaled"], st.batch(u) + 1)
                        for t in range(L.nt):
                            last = nc.tensor.matmul(bank[0:SQ, 0:E], OT[:, t, :], WO[:, E * t:E * t + E], start=t == 0, stop=t == L.nt - 1)
                        last.then_inc(S["product"], 1)

                    st = Stage(L, -1)
                    context_turn(st, -2, 0)
                    query_turn(st, -1)
                    pe.wait_ge(S["low_w"], 1)
                    keys(st, -1, range(L.nt))
                    pe.wait_ge(S["low_w"], 3)
                    queries(st, -1)
                    values(st, -1, range(L.nv))
                    context_turn(st, -1, 1)
                    pe.wait_ge(wo_in[nm], wo_parts[nm])

                    def body(st):
                        for u in range(2):
                            heads(st, u)
                            if st.has_pair(u):
                                query_turn(st, u)
                            if st.has_next(u):
                                values(st, u, range(L.nv - 2))
                            spread(st, u)
                            if st.has_next(u):
                                values(st, u, range(L.nv - 2, L.nv))
                            if st.has_after(u):
                                context_turn(st, u, u)
                            if st.has_pair(u):
                                queries(st, u)
                            project(st, u)
                    loop(pe, body)

                @block.scalar
                def _(act):
                    act.sem_inc(S["exped"], 2)
                    act.sem_inc(S["unloaded_odd"], 1)

                    def split_high(c):
                        act.wait_ge(w_in[nm][c], 16)
                        nc.scalar.activation(wsplit(WH, c), wraw(c), ACT.Copy).then_inc(S["high_w"], 1)

                    def take(st, key, dst, rows, n, scale=1.0, bias=None):
                        act.wait_ge(S["product"], st.jobs.upto(key))
                        src = PJ[st.jobs.slot(key)][0:rows, 0:n]
                        if bias is None and scale == 1.0:
                            return nc.scalar.activation(dst, src, ACT.Copy)
                        return nc.scalar.activation(dst, src, ACT.Identity, bias=0.0 if bias is None else bias, scale=scale)

                    def to_split(st, key, n, **kw):
                        s = st.splits.upto(key)
                        if not isinstance(s, int) or s > 2:
                            act.wait_ge(S["split"], s - 2)
                        take(st, key, T32[:, st.splits.slot(key), 0:n], 128, n, **kw).then_inc(S["taken"], 1)

                    def context(st, u):
                        for k in range(KE):
                            kw = {"scale": col(nm + "cg", k), "bias": col(nm + "cb", k)} if L.ctx_norm else {}
                            to_split(st, ("ctx", u, k), SK, **kw)

                    def keys(st, u, todo):
                        for t in todo:
                            to_split(st, ("K", u, t), SKE, **({} if L.wide else {"bias": col(nm + "bk", t)}))

                    def query_turn(st, u):
                        for k in range(KE):
                            kw = {"scale": col("nw", k)} if nm == "L1" else {} if nm == "L2" else {"scale": col(nm + "xg", k), "bias": col(nm + "xb", k)}
                            to_split(st, ("xT", u, k), 2 * SQ, **kw)

                    def queries(st, u):
                        for t in range(L.nt):
                            to_split(st, ("Q", u, t), 2 * SQ, **({} if L.wide else {"bias": col(nm + "bq", t)}))

                    def values(st, u, todo):
                        if todo[0] == 0 and not st.first:
                            act.wait_ge(S["weighed"], st.head(u, H - 1) + 2)
                        for c in todo:
                            t, part = c % KV_TILES, c // KV_TILES
                            r = KV_ROWS[t]
                            if L.wide:
                                dst = V[0:r, t * L.hw + part * L.vn:t * L.hw + part * L.vn + L.vn]
                                take(st, ("V", u, c), dst, r, L.vn).then_inc(S["taken"], 1)
                            else:
                                act.wait_ge(S["product"], st.jobs.upto(("V", u, c)))
                                dst = V[0:r, t * L.hw:t * L.hw + L.hw].rearrange("p (h d) -> p h d", h=H)[:, :, 0:16]
                                src = PJ[st.jobs.slot(("V", u, c))][0:r, 0:L.vn].rearrange("p (h d) -> p h d", h=H)
                                nc.scalar.activation(dst, src, ACT.Copy).then_inc(S["taken"], 1)

                    def heads(st, u):
                        for s in range(H + UA):
                            if s < H:
                                act.wait_ge(S["maxed"], st.head(u, s))
                                act.wait_ge(S["turned"], st.head(u, s))
                                nc.scalar.activation(P[:, s % 4, 0:SK], scores_of(s)[0:SQ, 0:SK], ACT.Exp, bias=MX[:, u, s:s + 1],
                                                     scale=1.0, accum_out=DEN[:, u, s:s + 1]).then_inc(S["exped"], 1)
                            h = s - UA
                            if h >= 0 and h % 2 == 1:
                                act.wait_ge(S["turned"], st.head(u, h) + 4)
                                act.wait_ge(S["weighed"], st.of_three(u, h))
                                nc.scalar.activation(PT[:, h % 3, :], PP[h % 2][:, 0:KV_TILES * SQ], ACT.Copy).then_inc(S["unloaded_odd"], 1)
                            if st.has_next(u) and 1 < s <= H + 1 and s % L.per == 1:
                                keys(st, u, [s // L.per - 1])

                    def spread(st, u):
                        for r in range(L.nr):
                            act.wait_ge(S["product"], st.jobs.upto(("R", u, r)))
                            nc.scalar.activation(OT[:, 4 * r:4 * r + 4, :].rearrange("p t q -> p (t q)"),
                                                 PJ[st.jobs.slot(("R", u, r))][:, 0:4 * SQ], ACT.Copy).then_inc(S["taken"], 1)

                    st = Stage(L, -1)
                    split_high(0)
                    context(st, -2)
                    query_turn(st, -1)
                    split_high(1)
                    split_high(2)
                    keys(st, -1, range(L.nt))
                    queries(st, -1)
                    if not L.wide:
                        act.wait_ge(S["cleared_v"], 1)
                    values(st, -1, range(L.nv))
                    context(st, -1)

                    def body(st):
                        for u in range(2):
                            heads(st, u)
                            if st.has_pair(u):
                                query_turn(st, u)
                            if st.has_next(u):
                                values(st, u, range(L.nv - 2))
                            spread(st, u)
                            if st.has_next(u):
                                values(st, u, range(L.nv - 2, L.nv))
                            if st.has_after(u):
                                context(st, u)
                            if st.has_pair(u):
                                queries(st, u)
                            take(st, ("out", u, 0), Y[:, :], SQ, E).then_inc(S["taken"], 1)
                    loop(act, body)

                @block.vector
                def _(dve):
                    dve.sem_inc(S["unloaded_even"], 1)
                    dve.sem_inc(S["freed"], L.nr)
                    q_scale = {"L0": 0.25, "L1": 1.0, "L2": 0.125, "L3": 0.25}[nm]

                    def split_low(c):
                        dve.wait_ge(S["high_w"], c + 1)
                        nc.vector.tensor_tensor(wsplit(WL, c), wraw(c), wsplit(WH, c).bitcast(fp32), ALU.subtract).then_inc(S["low_w"], 1)

                    def stats(r, src, at, end=False):
                        last = nc.vector.bn_stats(BN[0:r, at, :], src)
                        if end:
                            last.then_inc(S["stats"], 1)

                    def moments(st, key, rows, at):
                        wait_apart(dve, S["stats"], st.norms.upto(key))
                        for n, r in enumerate(rows):
                            last = nc.vector.bn_aggr(MV[0:r, at + n, :], BN[0:r, at + n, :])
                        last.then_inc(S["moments"], 1)

                    def context_stats(st, u, t):
                        n = u % 2
                        if t == 0:
                            wait_apart(dve, s_c[n], 32 if st.first else st.i * 32 + 64)
                        stats(KV_ROWS[t], C[0:KV_ROWS[t], n, t, :], t, end=t == KV_TILES - 1)

                    def context_norm(st, u, t):
                        n, r = u % 2, KV_ROWS[t]
                        if t == 0:
                            dve.wait_ge(S["rstd"], st.norms.upto(("ctx", u)))
                        last = nc.vector.tensor_scalar(CN[0:r, t, :], C[0:r, n, t, :], MV[0:r, t, 0:1], RS[0:r, t:t + 1], ALU.subtract, ALU.mult)
                        if t == KV_TILES - 1:
                            last.then_inc(S["normed"], 1)

                    def x_rows(st, v):
                        b = v if st.first else st.i * 2 + 2 + v
                        return X[:, b, :]

                    def x_norm(st, u, v):
                        if v == 0:
                            dve.wait_ge(S["rstd"], st.norms.upto(("x", u)))
                        if nm == "L1":
                            last = nc.vector.tensor_scalar(XN[:, v, :], x_rows(st, v), RS[0:SQ, 4 + v:5 + v], None, ALU.mult)
                        else:
                            last = nc.vector.tensor_scalar(XN[:, v, :], x_rows(st, v), MV[0:SQ, 4 + v, 0:1], RS[0:SQ, 4 + v:5 + v], ALU.subtract, ALU.mult)
                        if v == 1:
                            last.then_inc(S["normed"], 1)

                    def x_copy(st, u, v):
                        last = nc.vector.tensor_copy(XN[:, v, :], x_rows(st, v))
                        if v == 1:
                            last.then_inc(S["copied"], 1)

                    def split(st, key, part=None):
                        kind, u, t = key
                        s, j = st.splits.upto(key), st.jobs.upto(key)
                        n = {"ctx": SK, "K": SKE}.get(kind, 2 * SQ)
                        hi, lo = {"ctx": (CTH, CTL), "xT": (XTH, XTL), "K": (KH, KL), "Q": (QH, QL)}[kind]
                        hi, lo = hi[:, t, 0:n], lo[:, t, 0:n]
                        src = T32[:, st.splits.slot(key), 0:n]
                        if L.rope and kind in "KQ":
                            src = AC[:, st.turns.slot(key), 0:n]
                            r = st.turns.upto(key)
                            dve.wait_ge(S["rotated"], r)
                            nc.vector.tensor_tensor(src, src, SH[:, st.turns.slot(key), 0:n], ALU.add).then_inc(S["joined"], 1)
                            dve.wait_ge(S["joined"], r)
                        else:
                            dve.wait_ge(S["taken"], j)
                        scale = q_scale if kind == "Q" else 1.0
                        narrow_key = kind == "K" and not L.wide
                        if narrow_key:
                            hi = KR[:, st.splits.slot(key), 0:n]
                        if part == "low":
                            pass
                        elif scale != 1.0:
                            nc.vector.tensor_scalar(hi, src, scale, None, ALU.mult).then_inc(S["rounded"], 1)
                        else:
                            nc.vector.tensor_copy(hi, src).then_inc(S["rounded"], 1)
                        if part == "high":
                            return
                        dve.wait_ge(S["rounded"], s)
                        if narrow_key:
                            nc.vector.scalar_tensor_tensor(out=KH[:, t, :], in0=hi.bitcast(fp32), scalar=low_half, in1=src,
                                                           op0=ALU.mult, op1=ALU.add).then_inc(S["split"], 1)
                        elif scale != 1.0:
                            nc.vector.scalar_tensor_tensor(out=lo, in0=src, scalar=scale, in1=hi.bitcast(fp32),
                                                           op0=ALU.mult, op1=ALU.subtract).then_inc(S["split"], 1)
                        else:
                            nc.vector.tensor_tensor(lo, src, hi.bitcast(fp32), ALU.subtract).then_inc(S["split"], 1)

                    def shuffle(st, key):
                        n = SKE if key[0] == "K" else 2 * SQ
                        wait_apart(dve, S["taken"], st.jobs.upto(key))
                        nc.vector.stream_shuffle(SH[:, st.turns.slot(key), 0:n], T32[:, st.splits.slot(key), 0:n],
                                                 [p ^ 1 for p in range(32)]).then_inc(S["shuffled"], 1)

                    def splits(st, todo):
                        if L.rope and todo[0][0] in "KQ":
                            shuffle(st, todo[0])
                            for this, then in zip(todo, todo[1:] + [None]):
                                if then:
                                    shuffle(st, then)
                                split(st, this)
                        else:
                            for key in todo:
                                split(st, key)

                    def heads(st, u):
                        for s in range(H + 5):
                            if s < H:
                                dve.wait_ge(S["scores"], st.head(u, s))
                                nc.vector.tensor_reduce(MX[:, u, s:s + 1], scores_of(s)[0:SQ, 0:SK], AX.X, ALU.max,
                                                        negate=True).then_inc(S["maxed"], 1)
                            h = s - UD
                            if 0 <= h < H and h % 2 == 0:
                                dve.wait_ge(S["turned"], st.head(u, h) + 4)
                                dve.wait_ge(S["weighed"], st.of_three(u, h))
                                nc.vector.tensor_copy(PT[:, h % 3, :], PP[h % 2][:, 0:KV_TILES * SQ]).then_inc(S["unloaded_even"], 1)
                            if st.has_next(u):
                                if L.rope and s % 2 == 0 and 0 <= s // 2 - 2 < L.nt:
                                    shuffle(st, ("K", u, s // 2 - 2))
                                t, part = divmod(s - L.per - (4 if L.rope else 3), L.per)
                                if 0 <= t < L.nt and part == 0:
                                    split(st, ("K", u, t))
                            if L.rope and u == 1:
                                if s == 1:
                                    finish(st, 0)
                                if s == 3:
                                    post(st, 0)
                            if L.ctx_norm and st.has_after(u):
                                if 1 <= s <= KV_TILES:
                                    context_stats(st, u, s - 1)
                                if s == 4:
                                    moments(st, ("ctx", u), KV_ROWS, 0)
                                if s in (8, 10, 12):
                                    context_norm(st, u, (s - 8) // 2)
                            if st.has_pair(u):
                                if L.x_norm:
                                    if s in (5, 6):
                                        stats(SQ, x_rows(st, s - 5), s - 1, end=s == 6)
                                    if s == 7:
                                        moments(st, ("x", u), [SQ, SQ], 4)
                                    if s in (14, 15):
                                        x_norm(st, u, s - 14)
                                elif s in (7, 8):
                                    x_copy(st, u, s - 7)
                            if s == H + 1:
                                invert(st, u)

                    def invert(st, u):
                        dve.wait_ge(S["exped"], st.head(u, H - 1) + 2)
                        nc.vector.reciprocal(RDEN[:, :], DEN[:, u, :]).then_inc(S["inverse"], 1)
                        dve.wait_ge(S["inverse"], st.batch(u) + 1)
                        nc.vector.tensor_copy(RX[:, 0:L.hw].rearrange("p (h r) -> p h r", h=H),
                                              RDEN[:, :].unsqueeze(2).to_broadcast([SQ, H, L.rows])).then_inc(S["repeated"], 1)

                    def scale(st, u):
                        for r in range(L.nr):
                            dve.wait_ge(S["taken"], st.jobs.upto(("R", u, r)))
                            o = OT[:, 4 * r:4 * r + 4, :].rearrange("p t q -> p (t q)")
                            last = nc.vector.tensor_tensor(o, PO[r][:, 0:4 * SQ], o, ALU.mult).then_inc(S["freed"], 1)
                        dve.wait_ge(S["freed"], (st.batch(u) + 2) * L.nr)
                        if L.wide:
                            dve.sem_inc(S["scaled"], 1)
                        else:
                            for t in range(L.nt):
                                last = nc.vector.tensor_scalar(OT[:, t, :], OT[:, t, :], col(nm + "bv", t), None, ALU.add)
                            last.then_inc(S["scaled"], 1)

                    def finish(st, u):
                        n = st.batch(u)
                        x = X[:, n, :]
                        dve.wait_ge(S["taken"], st.jobs.upto(("out", u, 0)))
                        if nm == "L1":
                            nc.vector.tensor_tensor(x, x, Y[:, :], ALU.add).then_inc(S["summed"], 1)
                            return
                        nc.vector.tensor_tensor(x, x, Y[:, :], ALU.add).then_inc(S["added"], 1)
                        wait_apart(dve, S["added"], n + 1)
                        if nm != "L2":
                            nc.vector.tensor_tensor(x, x, ROWS[:, 0 if nm == "L0" else 4, :], ALU.add).then_inc(S["summed"], 1)
                            return
                        stats(SQ, x, 3, end=True)
                        moments(st, ("post", u), [SQ], 3)

                    def post(st, u):
                        n = st.batch(u)
                        x = X[:, n, :]
                        dve.wait_ge(S["rstd"], st.norms.upto(("post", u)))
                        nc.vector.tensor_scalar(Y[:, :], x, MV[0:SQ, 3, 0:1], RS[0:SQ, 3:4], ALU.subtract, ALU.mult).then_inc(S["normed"], 1)
                        dve.wait_ge(S["normed"], st.norms.upto(("post", u)))
                        nc.vector.tensor_tensor(Y[:, :], Y[:, :], ROWS[:, 2, :], ALU.mult).then_inc(S["gammaed"], 1)
                        dve.wait_ge(S["gammaed"], n + 1)
                        nc.vector.tensor_tensor(x, Y[:, :], ROWS[:, 3, :], ALU.add).then_inc(S["summed"], 1)

                    st = Stage(L, -1)
                    def context_whole(st, u):
                        for t in range(KV_TILES):
                            context_stats(st, u, t)
                        moments(st, ("ctx", u), KV_ROWS, 0)
                        for t in range(KV_TILES):
                            context_norm(st, u, t)

                    if L.ctx_norm:
                        context_whole(st, -2)
                    for v in range(2):
                        if L.x_norm:
                            stats(SQ, x_rows(st, v), 4 + v, end=v == 1)
                        else:
                            x_copy(st, -1, v)
                    if L.x_norm:
                        moments(st, ("x", -1), [SQ, SQ], 4)
                        for v in range(2):
                            x_norm(st, -1, v)
                    split_low(0)
                    splits(st, [("ctx", -2, k) for k in range(KE)])
                    splits(st, [("xT", -1, k) for k in range(KE)])
                    split_low(1)
                    split_low(2)
                    splits(st, [("K", -1, t) for t in range(L.nt)])
                    if L.ctx_norm:
                        context_whole(st, -1)
                    splits(st, [("Q", -1, t) for t in range(L.nt)])
                    splits(st, [("ctx", -1, k) for k in range(KE)])

                    def body(st):
                        for u in range(2):
                            heads(st, u)
                            if st.has_pair(u):
                                splits(st, [("xT", u, k) for k in range(KE)])
                            scale(st, u)
                            if st.has_after(u):
                                splits(st, [("ctx", u, k) for k in range(KE)])
                            if st.has_pair(u):
                                splits(st, [("Q", u, t) for t in range(L.nt)])
                            if not (L.rope and u == 0):
                                finish(st, u)
                                if L.rope:
                                    post(st, u)
                    loop(dve, body)

                @block.gpsimd
                def _(pool):
                    if not L.wide:
                        nc.gpsimd.memset(WO[:, 0:4 * E], 0.0).then_inc(S["cleared_w"], 1)
                        nc.gpsimd.memset(V[:, 0:KV_TILES * L.hw], 0.0).then_inc(S["cleared_v"], 1)

                    def rstd(st, key, at, n, eps):
                        m = st.norms.upto(key)
                        wait_apart(pool, S["moments"], m)
                        ve, mean, var = VE[:, at:at + n], MV[:, at:at + n, 0], MV[:, at:at + n, 1]
                        if nm == "L1":
                            nc.gpsimd.tensor_tensor(ve, mean, mean, ALU.mult).then_inc(S["square"], 1)
                            pool.wait_ge(S["square"], m)
                            nc.gpsimd.tensor_tensor(SQV[:, at:at + n], ve, var, ALU.add).then_inc(S["squares"], 1)
                            wait_apart(pool, S["squares"], m)
                            var = SQV[:, at:at + n]
                        nc.gpsimd.tensor_scalar(EV[:, at:at + n], var, eps, None, ALU.add).then_inc(S["powers"], 1)
                        pool.wait_ge(S["powers"], m)
                        nc.gpsimd.tensor_tensor(RS[:, at:at + n], EV[:, at:at + n], HALF[:, at:at + n], ALU.pow).then_inc(S["rstd"], 1)

                    def tables(st, u):
                        slot = 0 if st.first else 1 - u
                        n = 1 if st.first else st.batch(u) + 2
                        wait_apart(pool, s_m[slot], 16 if st.first else st.i * 16 + 16 * (u + 1))
                        nc.gpsimd.tensor_copy(MF[:, :], M8[:, slot, :]).then_inc(S["mask_float"], 1)
                        wait_apart(pool, S["mask_float"], n)
                        nc.gpsimd.tensor_tensor(COSM[:, :], cos, MF[:, :], ALU.mult)
                        nc.gpsimd.tensor_tensor(SINM[:, :], sin, MF[:, :], ALU.mult)
                        nc.gpsimd.tensor_scalar(MNEG[:, slot, :], MF[0:2, :], -1.0, None, ALU.add).then_inc(S["mask_tables"], 1)
                        wait_apart(pool, S["mask_tables"], n)

                    def rotate(st, todo):
                        for key in todo:
                            r, slot, keys = st.turns.upto(key), st.turns.slot(key), key[0] == "K"
                            src = T32[:, st.splits.slot(key), 0:SKE if keys else 2 * SQ]
                            ac, sh, c, s = AC[:, slot, :], SH[:, slot, :], COSM[:, :], SINM[:, :]
                            if not keys:
                                src, ac, sh = [x[:, 0:2 * SQ].rearrange("p (v q) -> p v q", v=2) for x in (src, ac, sh)]
                                c, s = [x[:, 0:SQ].unsqueeze(1).to_broadcast([128, 2, SQ]) for x in (cos, sin)]
                            pool.wait_ge(S["shuffled"], r)
                            nc.gpsimd.tensor_tensor(ac, src, c, ALU.mult)
                            nc.gpsimd.tensor_tensor(sh, sh, s, ALU.mult).then_inc(S["rotated"], 1)

                    def stand_alone(st, u):
                        for v in range(2):
                            for t in range(L.nt):
                                pool.wait_ge(S["split"], st.splits.upto(("Q", u, t)))
                                for Q_, A in zip((QH, QL), QA):
                                    last = nc.gpsimd.tensor_tensor(A[:, v, 4 * t:4 * t + 4, :],
                                                                   Q_[:, t, SQ * v:SQ * v + SQ].bitcast(fp32).unsqueeze(1).to_broadcast([128, 4, SQ]),
                                                                   own.unsqueeze(2).to_broadcast([128, 4, SQ]), ALU.mult)
                                last.then_inc(S["masked"], 1)

                    def segment(st, u):
                        if L.rope and st.has_next(u):
                            tables(st, u)
                        if L.ctx_norm and st.has_after(u):
                            rstd(st, ("ctx", -2 if st.first else u), 0, KV_TILES, L.eps)
                        if L.x_norm and st.has_pair(u):
                            rstd(st, ("x", u), 4, 2, L.eps)
                        if L.ctx_norm and st.first:
                            rstd(st, ("ctx", u), 0, KV_TILES, L.eps)
                        if L.rope and u == 1:
                            rstd(st, ("post", 0), 3, 1, L.eps_post)
                        if L.rope and st.has_next(u):
                            rotate(st, [("K", u, t) for t in range(L.nt)])
                        if L.rope and st.has_pair(u):
                            rotate(st, [("Q", u, t) for t in range(L.nt)])
                        if L.eps_post is not None and u == 1:
                            rstd(st, ("post", u), 3, 1, L.eps_post)

                        if not L.wide and st.has_pair(u):
                            stand_alone(st, u)

                    segment(Stage(L, -1), -1)

                    def body(st):
                        for u in range(2):
                            segment(st, u)
                    loop(pool, body)

        def feed_forward():
            G = 4
            nf = FF // 128
            per = KE + nf + G
            YN = RX[:, :].rearrange("p (g e) -> p g e", g=G)
            YH, YL = [K_[:, :, :].rearrange("p t n -> p (t n)")[:, 0:KE * G * SQ].rearrange("p (k n) -> p k n", k=KE) for K_ in (KH, KL)]
            HT = V[:, 0:nf * G * SQ].rearrange("p (t n) -> p t n", t=nf)
            FB = PJ
            assert per % 2 == 0
            nb = len(FB)
            TB = [FB[k] for k in range(KE)]
            with nc.Block() as block:

                @block.sync
                def _(sp):
                    load_output_weights(sp, "ffn")
                    sp.wait_ge(S["low_w"], 1)
                    load_weights(sp, "L1")

                @block.tensor
                def _(pe):
                    pe.sem_inc(S["taken"], nb)
                    with pe.Fori(0, B // G) as i:
                        pe.wait_ge(S["normed"], i + 1)
                        for k in range(KE):
                            pe.wait_ge(S["taken"], i * per + (k + 1))
                            for g in range(G):
                                last = nc.tensor.transpose(TB[k][:, SQ * g:SQ * g + SQ], YN[:, g, 128 * k:128 * k + 128], ident[0:SQ, 0:SQ])
                            last.then_inc(S["product"], 1)
                        pe.wait_ge(S["low_w"], 1)
                        pe.wait_ge(S["split"], (i + 1) * KE)
                        for t in range(nf):
                            n = KE + t
                            pe.wait_ge(S["taken"], i * per + (n + 1))
                            todo = [x for k in range(KE) for lh, ll in [[W[:, FF * k + 128 * t:FF * k + 128 * t + 128] for W in (WH, WL)]]
                                    for x in ((lh, YH[:, k, :]), (lh, YL[:, k, :]), (ll, YH[:, k, :]))]
                            for m, (x, y) in enumerate(todo):
                                last = nc.tensor.matmul(FB[n % nb][:, 0:G * SQ], x, y, start=m == 0, stop=m == len(todo) - 1)
                            last.then_inc(S["product"], 1)
                        pe.wait_ge(wo_in["ffn"], 16)
                        pe.wait_ge(S["taken"], i * per + (KE + nf + nb))
                        for g in range(G):
                            n = KE + nf + g
                            pe.wait_ge(S["taken"], i * per + (n + 1))
                            for t in range(nf):
                                last = nc.tensor.matmul(FB[n % nb][0:SQ, 0:E], HT[:, t, SQ * g:SQ * g + SQ], WO[:, E * t:E * t + E],
                                                        start=t == 0, stop=t == nf - 1)
                            last.then_inc(S["product"], 1)

                @block.scalar
                def _(act):
                    act.wait_ge(w_in["ffn"][0], 16)
                    nc.scalar.activation(WH[:, 0:KE * FF], W_RAW[:, 0, :], ACT.Copy).then_inc(S["high_w"], 1)
                    with act.Fori(0, B // G) as i:
                        for k in range(KE):
                            act.wait_ge(S["product"], i * per + (k + 1))
                            nc.scalar.activation(T32[:, k, :], TB[k][:, 0:G * SQ], ACT.Identity, bias=col("b2n", k),
                                                 scale=col("g2", k)).then_inc(S["taken"], 1)
                        for t in range(nf):
                            act.wait_ge(S["product"], i * per + (KE + t + 1))
                            nc.scalar.activation(HT[:, t, :], FB[(KE + t) % nb][:, 0:G * SQ], ACT.Gelu, bias=col("b1", t)).then_inc(S["taken"], 1)
                        for g in range(G):
                            n = KE + nf + g
                            act.wait_ge(S["product"], i * per + (n + 1))
                            nc.scalar.activation(P[:, g, 0:E], FB[n % nb][0:SQ, 0:E], ACT.Copy).then_inc(S["taken"], 1)

                @block.vector
                def _(dve):
                    dve.wait_ge(S["high_w"], 1)
                    nc.vector.tensor_tensor(WL[:, 0:KE * FF], W_RAW[:, 0, :], WH[:, 0:KE * FF].bitcast(fp32), ALU.subtract).then_inc(S["low_w"], 1)
                    with dve.Fori(0, B // G) as i:
                        for g in range(G):
                            last = nc.vector.bn_stats(BN[0:SQ, g, :], X[:, i * G + g, :])
                        last.then_inc(S["stats"], 1)
                        wait_apart(dve, S["stats"], i + 1)
                        for g in range(G):
                            last = nc.vector.bn_aggr(MV[0:SQ, g, :], BN[0:SQ, g, :])
                        last.then_inc(S["moments"], 1)
                        dve.wait_ge(S["rstd"], i + 1)
                        for g in range(G):
                            last = nc.vector.tensor_scalar(YN[:, g, :], X[:, i * G + g, :], MV[0:SQ, g, 0:1], RS[0:SQ, g:g + 1], ALU.subtract, ALU.mult)
                        last.then_inc(S["normed"], 1)
                        for k in range(KE):
                            dve.wait_ge(S["taken"], i * per + (k + 1 + nb))
                            nc.vector.tensor_copy(YH[:, k, :], T32[:, k, :]).then_inc(S["rounded"], 1)
                            dve.wait_ge(S["rounded"], i * KE + (k + 1))
                            nc.vector.tensor_tensor(YL[:, k, :], T32[:, k, :], YH[:, k, :].bitcast(fp32), ALU.subtract).then_inc(S["split"], 1)
                        for g in range(G):
                            x = X[:, i * G + g, :]
                            dve.wait_ge(S["taken"], i * per + (KE + nf + g + 1 + nb))
                            nc.vector.tensor_tensor(x, x, P[:, g, 0:E], ALU.add).then_inc(S["added"], 1)
                            dve.wait_ge(S["added"], i * G + (g + 1))
                            nc.vector.tensor_tensor(x, x, ROWS[:, 1, :], ALU.add).then_inc(S["summed"], 1)

                @block.gpsimd
                def _(pool):
                    with pool.Fori(0, B // G) as i:
                        wait_apart(pool, S["moments"], i + 1)
                        nc.gpsimd.tensor_scalar(EV[:, :], MV[:, :, 1], 1e-5, None, ALU.add).then_inc(S["powers"], 1)
                        pool.wait_ge(S["powers"], i + 1)
                        nc.gpsimd.tensor_tensor(RS[:, :], EV[:, :], HALF[:, :], ALU.pow).then_inc(S["rstd"], 1)

        for ph, what in enumerate(PHASES):
            if ph:
                clear_semaphores()
            if what == "ffn":
                feed_forward()
            else:
                attention(what, ph)


def constants():
    import numpy as np
    c = np.zeros((128, C_END), np.float32)
    c[:, C_ID:C_ID + 128] = np.eye(128)
    d = np.arange(128) % 64
    inv = (1.0 / np.float32(10000.0) ** (((d // 2) * 2).astype(np.float32) / np.float32(64))).astype(np.float32)
    ang = (np.arange(SKE, dtype=np.float32)[None, :] * inv[:, None]).astype(np.float32).astype(np.float64)
    c[:, C_COS:C_COS + SKE] = np.cos(ang)
    c[:, C_SIN:C_SIN + SKE] = np.sin(ang) * np.where(d % 2 == 0, -1.0, 1.0)[:, None]
    c[np.arange(128), C_OWN + np.arange(128) // 32] = 1.0
    c[:, C_NEG] = np.where(np.arange(128) % 32 >= 16, -1.0, 0.0)
    high = float(int(NEG) >> 18 << 18)
    c[0, C_FILL:C_FILL + SQ], c[1, C_FILL:C_FILL + SQ] = high, NEG - high
    return c


def vectors(a):
    import numpy as np
    out = np.zeros((128, VEC_END), np.float32)

    def tiles(name, src):
        v = np.asarray(a[src]).reshape(-1, 128)
        for k in range(v.shape[0]):
            out[:, VEC_COLS[name] + k] = v[k]
    for p, names in (("L0", ("ln1_g", "ln1_b", "ln1_g", "ln1_b")), ("L3", ("gkv", "betakv", "gq", "betaq"))):
        for v, src in zip(("cg", "cb", "xg", "xb"), names):
            tiles(p + v, f"{p}_xattn_{src}")
        for v in ("bq", "bk", "bv"):
            h = np.asarray(a[f"{p}_xattn_{v}"]).reshape(4, 4, 16)
            for t in range(4):
                for g in range(4):
                    for twice in range(1 if v == "bv" else 2):
                        r = 32 * g + 16 * twice
                        out[r:r + 16, VEC_COLS[p + v] + t] = h[t, g]
    for v, src in (("g2", "L0_xattn_ln2_g"), ("b2n", "L0_xattn_ln2_b"), ("b1", "L0_xattn_b1"), ("nw", "L1_xattn_norm_w")):
        tiles(v, src)
    return out


def kernel(**inputs):
    import numpy as np
    import concourse.bacc as bacc
    from concourse.bass_utils import run_bass_kernel_spmd

    nc = bacc.Bacc("TRN2", target_bir_lowering=False, num_devices=1)
    arrays, args = {}, {}
    for name, value in inputs.items():
        v = np.ascontiguousarray(value)
        short = "mask" if name == "mask_BxS2_bf1" else name
        if short == "mask":
            v = v.view(np.uint8)
        arrays[f"in_{short}"] = v
        args[short] = nc.dram_tensor(f"in_{short}", v.shape, mybir.dt.from_np(v.dtype), kind="ExternalInput").ap()
    arrays["vectors"] = vectors(inputs)
    args["vectors"] = nc.dram_tensor("vectors", (128, VEC_END), fp32, kind="ExternalInput").ap()
    arrays["constants"] = constants()
    consts = nc.dram_tensor("constants", (128, C_END), fp32, kind="ExternalInput").ap()
    out = nc.dram_tensor("out", (B, SQ, E), fp32, kind="ExternalOutput").ap()
    build(nc, args, consts, out)
    r = run_bass_kernel_spmd(nc, [{**arrays}], core_ids=[0])
    return r.results[0]["out"]
```

```python
import concourse.bass as bass
from concourse import mybir
from contextlib import ExitStack

fp32 = mybir.dt.float32
f32r = mybir.dt.float32r
u8 = mybir.dt.uint8
ALU = mybir.AluOpType
ACT = mybir.ActivationFunctionType
AX = mybir.AxisListType

B, SQ, SK, E, H = 16, 100, 361, 256, 16
KE = E // 128
KV_TILES = -(-SK // 128)
KV_ROWS = [min(128, SK - 128 * t) for t in range(KV_TILES)]
SKP = 128 * KV_TILES
SKE = SK + SK % 2
PAIRS = B // 2
FF = 4 * E
NEG = 1.0e9

C_ID, C_COS, C_SIN, C_NEG = 0, 128, 128 + SKE, 128 + 2 * SKE
C_FILL, C_OWN = C_NEG + 1, C_NEG + 1 + SQ
C_END = C_OWN + 4


VEC_COLS, VEC_END = {}, 0
for _p in ("L0", "L3"):
    for _v, _n in (("cg", KE), ("cb", KE), ("xg", KE), ("xb", KE), ("bq", 4), ("bk", 4), ("bv", 4)):
        VEC_COLS[_p + _v], VEC_END = VEC_END, VEC_END + _n
for _v, _n in (("g2", KE), ("b2n", KE), ("b1", FF // 128), ("nw", KE)):
    VEC_COLS[_v], VEC_END = VEC_END, VEC_END + _n


class Layer:

    def __init__(self, name, hd, ctx_norm, x_norm, rope, eps, eps_post=None):
        self.name, self.hd, self.ctx_norm, self.x_norm, self.rope = name, hd, ctx_norm, x_norm, rope
        self.eps, self.eps_post = eps, eps_post
        self.wide = hd == 64
        self.rows = 64 if self.wide else 32
        self.per = 128 // self.rows
        self.nt = H // self.per
        self.k_parts = 2 if self.wide else 3
        self.hw = self.rows * H
        self.vn = 512 if self.wide else 256
        self.nv = KV_TILES * (hd * H // self.vn)
        self.nr = -(-self.nt // 4)


class Steps:

    def __init__(self, keys, base, parity=0):
        self.at = {k: n for n, k in enumerate(keys)}
        assert len(self.at) == len(keys)
        self.base, self.parity, self.count = base, parity, len(keys)

    def upto(self, key):
        return self.base + (self.at[key] + 1)

    def upto_or_before(self, key):
        return self.base if key[0] in ("out", "post") and key[1] < 0 else self.upto(key)

    def slot(self, key):
        return (self.parity + self.at[key]) % 2

    def before(self, u):
        return self.base + sum(1 for k in self.at if k[1] < u)


class Stage:

    def __init__(self, L, i, last=False):
        self.i, self.last, self.first = i, last, isinstance(i, int) and i < 0
        self.L, self.begin = L, isinstance(i, int) and i == 0
        jobs0 = self.jobs_of(L, -1, False)
        jobs1 = self.jobs_of(L, 0, False)
        splits0, splits1 = [[k for k in j if k[0] in ("ctx", "K", "xT", "Q")] for j in (jobs0, jobs1)]
        norms0, norms1 = self.norms_of(L, -1, False), self.norms_of(L, 0, False)
        assert len(jobs1) % 2 == 0 and len(splits1) % 2 == 0
        jobs = self.jobs_of(L, -1 if self.first else 0, last)
        splits = [k for k in jobs if k[0] in ("ctx", "K", "xT", "Q")]
        norms = self.norms_of(L, -1 if self.first else 0, last)

        def base(a, b):
            return 0 if self.first else len(a) + i * len(b)
        self.jobs = Steps(jobs, base(jobs0, jobs1), 0 if self.first else len(jobs0) % 2)
        self.splits = Steps(splits, base(splits0, splits1), 0 if self.first else len(splits0) % 2)
        self.norms = Steps(norms, base(norms0, norms1))
        turns0, turns1, turns = [[k for k in j if k[0] in "KQ"] for j in (jobs0, jobs1, jobs)]
        assert len(turns1) % 2 == 0
        self.turns = Steps(turns, base(turns0, turns1), 0 if self.first else len(turns0) % 2)

    def has_next(self, u):
        return not (self.last and u == 1)

    def has_after(self, u):
        return not self.last

    def has_pair(self, u):
        return self.first or (u == 1 and not self.last)

    def keys_split(self, u, t):
        if u == 0:
            return self.splits.base - (KE + self.L.nt - 1 - t)
        if u == 2:
            return self.splits.upto(("Q", -1 if self.first else 1, t))
        return self.splits.upto(("K", 0, self.L.nt - 1))

    def values_taken(self, u):
        return self.jobs.base if u == 0 else self.jobs.upto(("V", 0, self.L.nv - 1))

    def context_split(self, u):
        return self.splits.before(u)

    @staticmethod
    def jobs_of(L, i, last):
        if i < 0:
            return ([("ctx", -2, k) for k in range(KE)] + [("xT", -1, k) for k in range(KE)]
                    + [("K", -1, t) for t in range(L.nt)] + [("Q", -1, t) for t in range(L.nt)]
                    + [("V", -1, c) for c in range(L.nv)] + [("ctx", -1, k) for k in range(KE)])
        out = []
        for u in range(2):
            if not (last and u == 1):
                out += [("K", u, t) for t in range(L.nt)]
            out += [k for k in Stage.tail_of(L, u, last) if k[0] != "S"]
            out.append(("out", u, 0))
        return out

    @staticmethod
    def tail_of(L, u, last):
        nxt, pair = not (last and u == 1), u == 1 and not last
        out, q = [], 0
        for c in range(L.nv):
            if c == L.nv - L.nr:
                out += [("R", u, r) for r in range(L.nr)]
            if nxt:
                out.append(("V", u, c))
            if pair and c == 0:
                out += [("xT", u, k) for k in range(KE)]
            if pair and 1 <= c < L.nv - 1:
                out += [("Q", u, t) for t in range(q, q + L.nt // (L.nv - 2))]
                q += L.nt // (L.nv - 2)
        for k in range(KE):
            if not last:
                out.append(("ctx", u, k))
            if nxt:
                out.append(("S", u, k))
        return out

    def tail(self, u):
        return self.tail_of(self.L, u, self.last)

    @staticmethod
    def norms_of(L, i, last):
        if i < 0:
            return ([("ctx", -2)] if L.ctx_norm else []) + ([("x", -1)] if L.x_norm else []) + ([("ctx", -1)] if L.ctx_norm else [])
        out = []
        for u in range(2):
            if L.ctx_norm and not last:
                out.append(("ctx", u))
            if L.x_norm and u == 1 and not last:
                out.append(("x", u))
            if L.eps_post is not None:
                out.append(("post", u))
        return out

    def pair(self):
        return 1 if self.first else self.i + 2

    def batch(self, u):
        return self.i * 2 + u

    def own(self, u, t):
        return self.i * 8 + (4 * u + t + 1)

    def half_head(self, u, h):
        return self.i * H + (H // 2 * u + h // 2 + 1)

    def of_three(self, u, h):
        return self.head(u, max(h, 2)) - 1

    def head(self, u, h):
        return self.i * (2 * H) + (H * u + h + 1)


PASSED = []


def wait_apart(eng, s, value):
    eng.wait_ge(s, value)
    eng.sem_inc(PASSED[0], 1)


def build(nc, a, consts, out):
    stack = ExitStack()
    with stack:
        def sb(name, shape, dt=fp32):
            return stack.enter_context(nc.sbuf_tensor(name, shape, dt))

        def ps(name, shape):
            return stack.enter_context(nc.psum_tensor(name, shape, fp32))

        def sem(name):
            return stack.enter_context(nc.semaphore(name))

        X = sb("X", [SQ, B, E])
        CON = sb("CON", [128, C_END])
        ident = CON[:, C_ID:C_ID + 128]
        cos, sin = CON[:, C_COS:C_COS + SKE], CON[:, C_SIN:C_SIN + SKE]
        low_half = CON[:, C_NEG:C_NEG + 1]
        own = CON[:, C_OWN:C_OWN + 4]
        VEC = sb("VEC", [128, VEC_END])
        ROWS = sb("ROWS", [SQ, 5, E])
        W_RAW = sb("W_RAW", [128, 3, 2048])
        WH = sb("WH", [128, 6144], f32r)
        WL = sb("WL", [128, 6144], f32r)
        WO = sb("WO", [128, 2048])
        C = sb("C", [128, 2, KV_TILES, E])
        CTH, CTL = sb("CTH", [128, KE, SKE], f32r), sb("CTL", [128, KE, SKE], f32r)
        KH, KL = sb("KH", [128, 8, SKE], f32r), sb("KL", [128, 8, SKE], f32r)
        KR = KL[:, 0:2, :]
        V = sb("V", [128, 3200])
        QH, QL = sb("QH", [128, 8, 2 * SQ], f32r), sb("QL", [128, 8, 2 * SQ], f32r)
        T32 = sb("T32", [128, 2, 4 * SQ])
        WORK = sb("WORK", [128, 7 * SKE])
        CN = WORK[:, 0:KV_TILES * E].rearrange("p (t e) -> p t e", e=E)
        SH, AC = [WORK[:, n * SKE:(n + 2) * SKE].rearrange("p (s n) -> p s n", s=2) for n in (0, 2)]
        COSM, SINM, MF = [WORK[:, n * SKE:(n + 1) * SKE] for n in (4, 5, 6)]
        M8 = sb("M8", [128, 2, SKE], u8)
        MNEG = sb("MNEG", [128, 2, SKE], f32r)
        FILL = sb("FILL", [128, SQ], f32r)
        XN = sb("XN", [SQ, 2, E])
        XTH, XTL = sb("XTH", [128, KE, 2 * SQ], f32r), sb("XTL", [128, KE, 2 * SQ], f32r)
        P = sb("P", [SQ, 4, SKP])
        PT = sb("PT", [128, 3, KV_TILES * SQ])
        RX = sb("RX", [SQ, H * 64])
        OT = sb("OT", [128, 8, SQ])
        Y = sb("Y", [SQ, E])
        MX = sb("MX", [SQ, 2, H])
        DEN = sb("DEN", [SQ, 2, H])
        RDEN = sb("RDEN", [SQ, H])
        BN = sb("BN", [128, 6, 6])
        MV = sb("MV", [128, 6, 2])
        VE = sb("VE", [128, 6])
        EV = sb("EV", [128, 6])
        SQV = sb("SQV", [128, 6])
        RS = sb("RS", [128, 6])
        HALF = sb("HALF", [128, 6])

        PJ = [ps(f"PJ{n}", [128, 512]) for n in range(2)]
        PS_ = [ps(f"PS{n}", [128, 512]) for n in range(2)]
        PP = [ps(f"PP{n}", [128, 512]) for n in range(2)]
        PO = [ps(f"PO{n}", [128, 512]) for n in range(2)]

        def col(name, k=0):
            c = VEC_COLS[name] + k
            return VEC[:, c:c + 1]

        LAYERS = [Layer("L0", 16, True, True, False, 1e-5), Layer("L1", 64, False, True, False, 1e-6),
                  Layer("L2", 64, False, False, True, None, 1e-3), Layer("L3", 16, True, True, False, 1e-5)]
        PHASES = [LAYERS[0], "ffn", LAYERS[1], LAYERS[2], LAYERS[3]]
        names = ["L0", "ffn", "L1", "L2", "L3"]
        w_in = {n: [sem(f"{n}_w{c}_in") for c in range(3)] for n in names}
        wo_in = {n: sem(f"{n}_wo_in") for n in names}
        wo_parts = {"L0": 64, "ffn": 16, "L1": 16, "L2": 16, "L3": 64}

        def raw(c, n):
            return W_RAW[:, c, 0:KE * n].rearrange("p (k n) -> p k n", k=KE)

        def load_weights(eng, n):
            if n == "ffn":
                eng.dma_start(raw(0, FF), a["L0_xattn_w1"].rearrange("(k p) n -> p k n", p=128)).then_inc(w_in[n][0], 16)
                return
            up = {"L0": "L0_xattn_w", "L1": "L1_xattn_w", "L2": "L2_xattn_W", "L3": "L3_xattn_W"}[n]
            width = 1024 if n in ("L1", "L2") else E
            for c, which in enumerate("kvq"):
                eng.dma_start(raw(c, width), a[up + which].rearrange("(k p) n -> p k n", p=128)).then_inc(w_in[n][c], 16)

        def load_output_weights(eng, n):
            if n == "ffn":
                src = a["L0_xattn_w2"]
            elif n in ("L1", "L2"):
                src = a["L1_xattn_wo" if n == "L1" else "L2_xattn_Wo"]
            else:
                src = a[n + ("_xattn_wo" if n == "L0" else "_xattn_Wo")].rearrange("(t g p) n -> g p t n", g=4, p=16)
                for g in range(4):
                    eng.dma_start(WO[32 * g:32 * g + 16, 0:4 * E].rearrange("p (t n) -> p t n", t=4),
                                  src[g]).then_inc(wo_in[n], 16)
                return
            eng.dma_start(WO[:, :].rearrange("p (t n) -> p t n", t=8),
                          src.rearrange("(t p) n -> p t n", p=128)).then_inc(wo_in[n], 16)

        def load_context(eng, n, slot, s_in):
            eng.dma_start(C[:, slot, 0:2, :], a["ctx_1024"][n, 0:256, :].rearrange("(t p) f -> p t f", p=128)).then_inc(s_in[slot], 16)
            eng.dma_start(C[0:KV_ROWS[2], slot, 2, :], a["ctx_1024"][n, 256:SK, :]).then_inc(s_in[slot], 16)

        s_c = [sem(f"context{n}_in") for n in range(2)]
        s_con, s_x, s_vec, s_rows = sem("con_in"), sem("x_in"), sem("vectors_in"), sem("rows_in")
        with nc.Block() as block:
            row_src = ["L0_xattn_bo", "L0_xattn_b2", "L2_xattn_ln_gamma", "L2_xattn_ln_beta", "L3_xattn_bo"]

            @block.sync
            def _(eng):
                load_context(eng, 0, 0, s_c)
                load_weights(eng, "L0")
                load_context(eng, 1, 1, s_c)
                eng.dma_start(X[:, :, :], a["x"].rearrange("b s f -> s b f")).then_inc(s_x, 16)
                for r, src in enumerate(row_src):
                    eng.dma_start(ROWS[:, r, :], a[src].rearrange("(o n) -> o n", o=1).broadcast_to([SQ, E])).then_inc(s_rows, 16)
                eng.wait_ge(s_x, 16)

            @block.scalar
            def _(eng):
                eng.dma_start(CON[:, :], consts).then_inc(s_con, 16)
                eng.dma_start(VEC[:, :], a["vectors"]).then_inc(s_vec, 16)
                eng.wait_ge(s_vec, 16)
                eng.wait_ge(s_con, 16)

            @block.vector
            def _(eng):
                eng.memset(HALF[:, :], -0.5)
                eng.memset(MV[:, :, :], 1.0)
                eng.memset(M8[:, :, SK:SKE], 0)
                for half in (CTH, CTL):
                    eng.memset(half[:, :, SK:SKE].bitcast(fp32), 0.0)
                eng.memset(P[:, :, SK:SKP], 0.0)
                eng.wait_ge(s_con, 16)
                eng.tensor_copy(FILL[:, :], CON[:, C_FILL:C_FILL + SQ])

        PASSED[:] = [sem("passed")]
        S = {k: sem(k) for k in
                 ("high_w", "low_w", "cleared_v", "cleared_w",
                  "product",
                  "taken",
                  "rounded",
                  "split",
                  "masked",
                  "scores", "maxed", "exped",
                  "turned", "unloaded_even", "unloaded_odd", "weighed",
                  "inverse", "repeated",
                  "bias_spread", "bias_made",
                  "scaled", "freed", "added", "summed",
                  "stats", "moments", "square", "squares", "powers", "rstd", "normed",
                  "copied", "shuffled", "rotated", "joined", "mask_float", "mask_tables", "gammaed")}
        s_m = [sem(f"mask{n}_in") for n in range(2)]
        s_out = sem("out_written")

        def clear_semaphores():
            with nc.Block() as block:

                @block.sync
                def _(sp):
                    for s in [*S.values(), *s_c, *s_m, *PASSED]:
                        sp.sem_clear(s)

        TL, UA, UD, PL = 2, 2, 2, 4
        LEAD = 2
        unloaded = ("unloaded_even", "unloaded_odd")

        def attention(L, ph):
            nm = L.name
            n_ = KE * L.hw
            wk, wv, wq = 0, n_, n_ + KE * L.hd * H
            vw = L.hd * H
            alone = KE * (2 * L.hw + L.hd * H)
            QA = None if L.wide else [W[:, alone:alone + 2 * H * SQ].rearrange("p (v h q) -> p v h q", v=2, h=H) for W in (WH, WL)]

            out_bias = 0 if nm == "L0" else 4

            def scores_of(h):
                return PS_[h % 2] if L.wide else [*PS_, PO[1]][h % 3]

            def wcols(c):
                at, w = ((wk, L.hw), (wv, vw), (wq, L.hw))[c]
                return at, w

            def wsplit(W, c):
                at, w = wcols(c)
                ap = W[:, at:at + KE * w]
                if L.wide or c == 1:
                    return ap
                return ap.rearrange("p (m d e) -> p m d e", d=2, e=16)

            def wraw(c):
                ap = W_RAW[:, c, 0:KE * vw]
                if L.wide or c == 1:
                    return ap
                return ap.rearrange("p (m e) -> p m e", e=16).unsqueeze(2).to_broadcast([128, KE * H, 2, 16])

            def w(W, c, k, n0, n1):
                at, width = wcols(c)
                return W[:, at + k * width + n0:at + k * width + n1]

            def loop(eng, body):
                with eng.Fori(0, PAIRS - 1) as i:
                    body(Stage(L, i))
                body(Stage(L, PAIRS - 1, last=True))

            with nc.Block() as block:

                @block.sync
                def _(sp):
                    for n in range(2):
                        if ph > 0:
                            load_context(sp, n, n, s_c)
                        if L.rope:
                            sp.dma_start(M8[:, n, 0:SK], a["mask"][n:n + 1, :].broadcast_to([128, SK])).then_inc(s_m[n], 16)
                    if not L.wide:
                        sp.wait_ge(S["cleared_w"], 1)
                    load_output_weights(sp, nm)
                    if ph < 4:
                        sp.wait_ge(S["low_w"], 3)
                        load_weights(sp, names[ph + 1])

                    def body(st):
                        for u in range(2):
                            if st.last:
                                continue
                            wait_apart(sp, S["scores"], st.head(u, 0))
                            load_context(sp, st.batch(u) + 2, u, s_c)
                            if L.rope:
                                wait_apart(sp, S["mask_tables"], st.batch(u) + 1)
                                n = st.batch(u) + 2
                                sp.dma_start(M8[:, u, 0:SK], a["mask"][bass.ds(n, 1), :].broadcast_to([128, SK])).then_inc(s_m[u], 16)
                    loop(sp, body)
                    if ph == 4:
                        sp.wait_ge(S["summed"], B + 1)
                        sp.dma_start(out.rearrange("b s f -> s b f"), X[:, :, :]).then_inc(s_out, 16)
                        sp.wait_ge(s_out, 16)

                @block.tensor
                def _(pe):
                    pe.sem_inc(S["turned"], 4)
                    pe.sem_inc(S["weighed"], 2)

                    def begin(st, key):
                        j = st.jobs.upto(key)
                        if not isinstance(j, int) or j > 2:
                            pe.wait_ge(S["taken"], j - 2)
                        return PJ[st.jobs.slot(key)]

                    def product3(dst, pairs, part=0, parts=1):
                        todo = [x for lh, ll, rh, rl in pairs for x in ((lh, rh), (lh, rl), (ll, rh))]
                        each = len(todo) // parts
                        for n, (l, r) in list(enumerate(todo))[each * part:each * part + each]:
                            last = nc.tensor.matmul(dst, l, r, start=n == 0, stop=n == len(todo) - 1)
                        return last

                    def context_turn(st, u, n, k):
                        if k == 0 and L.ctx_norm:
                            pe.wait_ge(S["normed"], st.norms.upto(("ctx", u)))
                        elif k == 0:
                            pe.wait_ge(s_c[n], 32 if st.first else st.i * 32 + 64)
                        src = CN if L.ctx_norm else C[:, n]
                        bank = begin(st, ("ctx", u, k))
                        for t, r in enumerate(KV_ROWS):
                            last = nc.tensor.transpose(bank[:, 128 * t:128 * t + r], src[0:r, t, 128 * k:128 * k + 128], ident[0:r, 0:r])
                        last.then_inc(S["product"], 1)

                    def keys(st, u, t, part=0, parts=1):
                        if t == 0 and part == 0:
                            pe.wait_ge(S["split"], st.splits.upto(("ctx", -2, KE - 1)) if st.first else st.context_split(u))
                        key = ("K", u, t)
                        bank = begin(st, key) if part == 0 else PJ[st.jobs.slot(key)]
                        last = product3(bank[:, 0:SKE], [(w(WH, 0, k, 128 * t, 128 * t + 128), w(WL, 0, k, 128 * t, 128 * t + 128),
                                                          CTH[:, k, :], CTL[:, k, :]) for k in range(KE)], part, parts)
                        if part == parts - 1:
                            last.then_inc(S["product"], 1)

                    def values(st, u, todo):
                        for c in todo:
                            t, part = c % KV_TILES, c // KV_TILES
                            r = KV_ROWS[t]
                            bank = begin(st, ("V", u, c))
                            product3(bank[0:r, 0:L.vn],
                                     [(CTH[:, k, 128 * t:128 * t + r], CTL[:, k, 128 * t:128 * t + r],
                                       w(WH, 1, k, L.vn * part, L.vn * part + L.vn), w(WL, 1, k, L.vn * part, L.vn * part + L.vn))
                                      for k in range(KE)]).then_inc(S["product"], 1)

                    def query_turn(st, u, k):
                        if k == 0 and L.x_norm:
                            pe.wait_ge(S["normed"], st.norms.upto(("x", u)))
                        elif k == 0:
                            pe.wait_ge(S["copied"], st.pair())
                        bank = begin(st, ("xT", u, k))
                        for v in range(2):
                            last = nc.tensor.transpose(bank[:, SQ * v:SQ * v + SQ], XN[:, v, 128 * k:128 * k + 128], ident[0:SQ, 0:SQ])
                        last.then_inc(S["product"], 1)

                    def queries(st, u, t):
                        if t == 0:
                            pe.wait_ge(S["split"], st.splits.upto(("xT", u, KE - 1)))
                        bank = begin(st, ("Q", u, t))
                        product3(bank[:, 0:2 * SQ], [(w(WH, 2, k, 128 * t, 128 * t + 128), w(WL, 2, k, 128 * t, 128 * t + 128),
                                                      XTH[:, k, :], XTL[:, k, :]) for k in range(KE)]).then_inc(S["product"], 1)

                    def scores(st, u, h):
                        t, r0, v = h // L.per, L.rows * (h % L.per), u % 2
                        if h == 0 or (u == 0 and L.wide and h % L.per == 0):
                            pe.wait_ge(S["split"], st.keys_split(u, t))
                        if h == 0 and L.rope:
                            pe.wait_ge(S["mask_tables"], st.batch(u) + 1)
                        pe.wait_ge(S["exped"], st.head(u, h) if L.wide else st.of_three(u, h))
                        q = slice(SQ * v, SQ * v + SQ)
                        if L.wide:
                            qh, ql = QH[r0:r0 + L.rows, t, q], QL[r0:r0 + L.rows, t, q]
                            kh, kl = KH[r0:r0 + L.rows, t, :], KL[r0:r0 + L.rows, t, :]
                            todo = [(qh, kh), (qh, kl), (ql, kh)]
                        else:
                            if h % L.per == 0:
                                pe.wait_ge(S["masked"], st.own(u, t))
                            todo = [(Q_[:, v, h, :], KH[:, t, :]) for Q_ in QA]
                        if L.rope:
                            todo = [(FILL[:, :], MNEG[:, v, :])] + todo
                        for n, (x, y) in enumerate(todo):
                            last = nc.tensor.matmul(scores_of(h)[0:SQ, 0:SKE], x, y, start=n == 0, stop=n == len(todo) - 1)
                        last.then_inc(S["scores"], 1)

                    def heads(st, u):
                        for s in range(H + PL):
                            if LEAD <= s < H:
                                scores(st, u, s)
                            t, part = divmod(s - L.per, L.per)
                            if st.has_next(u) and 0 <= t < L.nt and part < L.k_parts:
                                keys(st, u, t, part, L.k_parts)
                            if TL <= s < H + TL:
                                h = s - TL
                                pe.wait_ge(S["exped"], st.head(u, h) + 2)
                                pe.wait_ge(S[unloaded[h % 2]], st.half_head(u, h))
                                for t in range(KV_TILES):
                                    last = nc.tensor.transpose(PP[h % 2][:, SQ * t:SQ * t + SQ], P[:, h % 4, 128 * t:128 * t + 128], ident[0:SQ, 0:SQ])
                                last.then_inc(S["turned"], 1)
                            if s >= PL:
                                h = s - PL
                                t, r0 = h // L.per, L.rows * (h % L.per)
                                if h == 0:
                                    pe.wait_ge(S["taken"], st.values_taken(u))
                                    pe.wait_ge(S["freed"], (st.batch(u) + 1) * L.nr)
                                pe.wait_ge(S[unloaded[h % 2]], st.half_head(u, h) + 1)
                                for c, r in enumerate(KV_ROWS):
                                    last = nc.tensor.matmul(PO[t // 4][r0:r0 + L.rows, SQ * (t % 4):SQ * (t % 4) + SQ],
                                                            V[0:r, c * L.hw + L.rows * h:c * L.hw + L.rows * h + L.rows],
                                                            PT[0:r, h % 3, SQ * c:SQ * c + SQ], start=c == 0, stop=c == KV_TILES - 1)
                                last.then_inc(S["weighed"], 1)

                    def spread(st, u, r):
                        pe.wait_ge(S["repeated"], st.batch(u) + 1)
                        bank = begin(st, ("R", u, r))
                        for t in range(4):
                            c = 128 * (4 * r + t)
                            last = nc.tensor.transpose(bank[:, SQ * t:SQ * t + SQ], RX[:, c:c + 128], ident[0:SQ, 0:SQ])
                        last.then_inc(S["product"], 1)

                    def project(st, u):
                        bank = begin(st, ("out", u, 0))
                        pe.wait_ge(S["scaled"], st.batch(u) + 1)
                        for t in range(L.nt):
                            last = nc.tensor.matmul(bank[0:SQ, 0:E], OT[:, t, :], WO[:, E * t:E * t + E], start=t == 0, stop=t == L.nt - 1)
                        last.then_inc(S["product"], 1)

                    st = Stage(L, -1)
                    for k in range(KE):
                        context_turn(st, -2, 0, k)
                    for k in range(KE):
                        query_turn(st, -1, k)
                    pe.wait_ge(S["low_w"], 1)
                    for t in range(L.nt):
                        keys(st, -1, t)
                    pe.wait_ge(S["low_w"], 3)
                    for t in range(L.nt):
                        queries(st, -1, t)
                    values(st, -1, range(L.nv))
                    for k in range(KE):
                        context_turn(st, -1, 1, k)
                    for h in range(LEAD):
                        scores(st, 2, h)
                    pe.wait_ge(wo_in[nm], wo_parts[nm])
                    if not L.wide:
                        pe.wait_ge(S["bias_spread"], 1)
                        for t in range(L.nt):
                            last = nc.tensor.matmul(PO[0][0:SQ, 0:E], OT[:, t, :], WO[:, E * t:E * t + E], start=t == 0, stop=t == L.nt - 1)
                        last.then_inc(S["bias_made"], 1)

                    def body(st):
                        for u in range(2):
                            heads(st, u)
                            for kind, _, n in st.tail(u):
                                if kind == "V":
                                    values(st, u, [n])
                                elif kind == "xT":
                                    query_turn(st, u, n)
                                elif kind == "Q":
                                    queries(st, u, n)
                                elif kind == "R":
                                    spread(st, u, n)
                                elif kind == "ctx":
                                    context_turn(st, u, u, n)
                                elif kind == "S":
                                    scores(st, u + 1, n)
                            project(st, u)
                    loop(pe, body)

                @block.scalar
                def _(act):
                    act.sem_inc(S["exped"], 2)
                    act.sem_inc(S["unloaded_odd"], 1)

                    def split_high(c):
                        act.wait_ge(w_in[nm][c], 16)
                        nc.scalar.activation(wsplit(WH, c), wraw(c), ACT.Copy).then_inc(S["high_w"], 1)

                    def take(st, key, dst, rows, n, scale=1.0, bias=None):
                        act.wait_ge(S["product"], st.jobs.upto(key))
                        src = PJ[st.jobs.slot(key)][0:rows, 0:n]
                        if bias is None and scale == 1.0:
                            return nc.scalar.activation(dst, src, ACT.Copy)
                        return nc.scalar.activation(dst, src, ACT.Identity, bias=0.0 if bias is None else bias, scale=scale)

                    def to_split(st, key, n, **kw):
                        s = st.splits.upto(key)
                        if L.rope and key[0] in "KQ" and key[2] >= 2:
                            act.wait_ge(S["rotated"], st.turns.upto(key) - 2)
                        elif not isinstance(s, int) or s > 2:
                            act.wait_ge(S["split"], s - 2)
                        take(st, key, T32[:, st.splits.slot(key), 0:n], 128, n, **kw).then_inc(S["taken"], 1)

                    def context(st, u, k):
                        kw = {"scale": col(nm + "cg", k), "bias": col(nm + "cb", k)} if L.ctx_norm else {}
                        to_split(st, ("ctx", u, k), SK, **kw)

                    def keys(st, u, todo):
                        for t in todo:
                            to_split(st, ("K", u, t), SKE, **({} if L.wide else {"bias": col(nm + "bk", t)}))

                    def query_turn(st, u, k):
                        kw = {"scale": col("nw", k)} if nm == "L1" else {} if nm == "L2" else {"scale": col(nm + "xg", k), "bias": col(nm + "xb", k)}
                        to_split(st, ("xT", u, k), 2 * SQ, **kw)

                    def queries(st, u, t):
                        to_split(st, ("Q", u, t), 2 * SQ, **({} if L.wide else {"bias": col(nm + "bq", t)}))

                    def values(st, u, todo):
                        if 0 in todo and not st.first:
                            act.wait_ge(S["weighed"], st.head(u, H - 1) + 2)
                        for c in todo:
                            t, part = c % KV_TILES, c // KV_TILES
                            r = KV_ROWS[t]
                            if L.wide:
                                dst = V[0:r, t * L.hw + part * L.vn:t * L.hw + part * L.vn + L.vn]
                                take(st, ("V", u, c), dst, r, L.vn).then_inc(S["taken"], 1)
                            else:
                                act.wait_ge(S["product"], st.jobs.upto(("V", u, c)))
                                dst = V[0:r, t * L.hw:t * L.hw + L.hw].rearrange("p (h d) -> p h d", h=H)[:, :, 0:16]
                                src = PJ[st.jobs.slot(("V", u, c))][0:r, 0:L.vn].rearrange("p (h d) -> p h d", h=H)
                                nc.scalar.activation(dst, src, ACT.Copy).then_inc(S["taken"], 1)

                    def exponentials(st, u, h):
                        v = u % 2
                        act.wait_ge(S["maxed"], st.head(u, h))
                        act.wait_ge(S["turned"], st.head(u, h))
                        nc.scalar.activation(P[:, h % 4, 0:SK], scores_of(h)[0:SQ, 0:SK], ACT.Exp, bias=MX[:, v, h:h + 1],
                                             scale=1.0, accum_out=DEN[:, v, h:h + 1]).then_inc(S["exped"], 1)

                    def heads(st, u):
                        for s in range(H + 4):
                            if LEAD <= s < H:
                                exponentials(st, u, s)
                            h = s - UA
                            if 0 <= h < H and h % 2 == 1:
                                act.wait_ge(S["turned"], st.head(u, h) + 4)
                                act.wait_ge(S["weighed"], st.of_three(u, h))
                                nc.scalar.activation(PT[:, h % 3, :], PP[h % 2][:, 0:KV_TILES * SQ], ACT.Copy).then_inc(S["unloaded_odd"], 1)
                            t, part = divmod(s - L.per - L.k_parts, L.per)
                            if st.has_next(u) and 0 <= t < L.nt and part == 0:
                                keys(st, u, [t])

                    def spread(st, u, r):
                        act.wait_ge(S["product"], st.jobs.upto(("R", u, r)))
                        nc.scalar.activation(OT[:, 4 * r:4 * r + 4, :].rearrange("p t q -> p (t q)"),
                                             PJ[st.jobs.slot(("R", u, r))][:, 0:4 * SQ], ACT.Copy).then_inc(S["taken"], 1)

                    st = Stage(L, -1)
                    split_high(0)
                    for k in range(KE):
                        context(st, -2, k)
                    for k in range(KE):
                        query_turn(st, -1, k)
                    split_high(1)
                    split_high(2)
                    keys(st, -1, range(L.nt))
                    for t in range(L.nt):
                        queries(st, -1, t)
                    if not L.wide:
                        act.wait_ge(S["cleared_v"], 1)
                    values(st, -1, range(L.nv))
                    for k in range(KE):
                        context(st, -1, k)
                    for h in range(LEAD):
                        exponentials(st, 2, h)

                    def body(st):
                        for u in range(2):
                            heads(st, u)
                            for kind, _, n in st.tail(u):
                                if kind == "V":
                                    values(st, u, [n])
                                elif kind == "xT":
                                    query_turn(st, u, n)
                                elif kind == "Q":
                                    queries(st, u, n)
                                elif kind == "R":
                                    spread(st, u, n)
                                elif kind == "ctx":
                                    context(st, u, n)
                            if st.has_next(u):
                                for h in range(LEAD):
                                    exponentials(st, u + 1, h)
                            if not L.rope:
                                act.wait_ge(S["summed"], st.batch(u) + 1)
                            take(st, ("out", u, 0), Y[:, :], SQ, E).then_inc(S["taken"], 1)
                    loop(act, body)

                @block.vector
                def _(dve):
                    dve.sem_inc(S["unloaded_even"], 1)
                    dve.sem_inc(S["freed"], L.nr)
                    q_scale = {"L0": 0.25, "L1": 1.0, "L2": 0.125, "L3": 0.25}[nm]

                    def split_low(c):
                        dve.wait_ge(S["high_w"], c + 1)
                        nc.vector.tensor_tensor(wsplit(WL, c), wraw(c), wsplit(WH, c).bitcast(fp32), ALU.subtract).then_inc(S["low_w"], 1)

                    def stats(r, src, at, end=False):
                        last = nc.vector.bn_stats(BN[0:r, at, :], src)
                        if end:
                            last.then_inc(S["stats"], 1)

                    def moments(st, key, rows, at):
                        wait_apart(dve, S["stats"], st.norms.upto_or_before(key))
                        for n, r in enumerate(rows):
                            last = nc.vector.bn_aggr(MV[0:r, at + n, :], BN[0:r, at + n, :])
                        last.then_inc(S["moments"], 1)

                    def context_stats(st, u, t):
                        n = u % 2
                        if t == 0:
                            wait_apart(dve, s_c[n], 32 if st.first else st.i * 32 + 64)
                        stats(KV_ROWS[t], C[0:KV_ROWS[t], n, t, :], t, end=t == KV_TILES - 1)

                    def first_norm(st):
                        dve.wait_ge(S["rstd"], st.norms.upto(("ctx", -2)))
                        for t, r in enumerate(KV_ROWS):
                            last = nc.vector.tensor_scalar(CN[0:r, t, :], C[0:r, 0, t, :], MV[0:r, t, 0:1], RS[0:r, t:t + 1], ALU.subtract, ALU.mult)
                        last.then_inc(S["normed"], 1)

                    def x_rows(st, v):
                        b = v if st.first else st.i * 2 + 2 + v
                        return X[:, b, :]

                    def x_norm(st, u, v):
                        if v == 0:
                            dve.wait_ge(S["rstd"], st.norms.upto(("x", u)))
                        if nm == "L1":
                            last = nc.vector.tensor_scalar(XN[:, v, :], x_rows(st, v), RS[0:SQ, 4 + v:5 + v], None, ALU.mult)
                        else:
                            last = nc.vector.tensor_scalar(XN[:, v, :], x_rows(st, v), MV[0:SQ, 4 + v, 0:1], RS[0:SQ, 4 + v:5 + v], ALU.subtract, ALU.mult)
                        if v == 1:
                            last.then_inc(S["normed"], 1)

                    def x_copy(st, u, v):
                        last = nc.vector.tensor_copy(XN[:, v, :], x_rows(st, v))
                        if v == 1:
                            last.then_inc(S["copied"], 1)

                    def split(st, key, part=None):
                        kind, u, t = key
                        s, j = st.splits.upto(key), st.jobs.upto(key)
                        n = {"ctx": SK, "K": SKE}.get(kind, 2 * SQ)
                        hi, lo = {"ctx": (CTH, CTL), "xT": (XTH, XTL), "K": (KH, KL), "Q": (QH, QL)}[kind]
                        hi, lo = hi[:, t, 0:n], lo[:, t, 0:n]
                        src = T32[:, st.splits.slot(key), 0:n]
                        if L.rope and kind in "KQ":
                            src = AC[:, st.turns.slot(key), 0:n]
                            r = st.turns.upto(key)
                            dve.wait_ge(S["rotated"], r)
                            nc.vector.tensor_tensor(src, src, SH[:, st.turns.slot(key), 0:n], ALU.add).then_inc(S["joined"], 1)
                            dve.wait_ge(S["joined"], r)
                        else:
                            dve.wait_ge(S["taken"], j)
                        scale = q_scale if kind == "Q" else 1.0
                        narrow_key = kind == "K" and not L.wide
                        if narrow_key:
                            hi = KR[:, st.splits.slot(key), 0:n]
                        if part == "low":
                            pass
                        elif scale != 1.0:
                            nc.vector.tensor_scalar(hi, src, scale, None, ALU.mult).then_inc(S["rounded"], 1)
                        else:
                            nc.vector.tensor_copy(hi, src).then_inc(S["rounded"], 1)
                        if part == "high":
                            return
                        dve.wait_ge(S["rounded"], s)
                        if narrow_key:
                            nc.vector.scalar_tensor_tensor(out=KH[:, t, :], in0=hi.bitcast(fp32), scalar=low_half, in1=src,
                                                           op0=ALU.mult, op1=ALU.add).then_inc(S["split"], 1)
                        elif scale != 1.0:
                            nc.vector.scalar_tensor_tensor(out=lo, in0=src, scalar=scale, in1=hi.bitcast(fp32),
                                                           op0=ALU.mult, op1=ALU.subtract).then_inc(S["split"], 1)
                        else:
                            nc.vector.tensor_tensor(lo, src, hi.bitcast(fp32), ALU.subtract).then_inc(S["split"], 1)

                    def shuffle(st, key):
                        n = SKE if key[0] == "K" else 2 * SQ
                        wait_apart(dve, S["taken"], st.jobs.upto(key))
                        nc.vector.stream_shuffle(SH[:, st.turns.slot(key), 0:n], T32[:, st.splits.slot(key), 0:n],
                                                 [p ^ 1 for p in range(32)]).then_inc(S["shuffled"], 1)

                    def splits(st, todo):
                        if L.rope and todo[0][0] in "KQ":
                            shuffle(st, todo[0])
                            for this, then in zip(todo, todo[1:] + [None]):
                                if then:
                                    shuffle(st, then)
                                split(st, this)
                        else:
                            for key in todo:
                                split(st, key)

                    def maximum(st, u, h):
                        dve.wait_ge(S["scores"], st.head(u, h))
                        nc.vector.tensor_reduce(MX[:, u % 2, h:h + 1], scores_of(h)[0:SQ, 0:SK], AX.X, ALU.max,
                                                negate=True).then_inc(S["maxed"], 1)

                    def heads(st, u):
                        for s in range(H + 6):
                            if LEAD <= s < H:
                                maximum(st, u, s)
                            h = s - UD
                            if 0 <= h < H and h % 2 == 0:
                                dve.wait_ge(S["turned"], st.head(u, h) + 4)
                                dve.wait_ge(S["weighed"], st.of_three(u, h))
                                nc.vector.tensor_copy(PT[:, h % 3, :], PP[h % 2][:, 0:KV_TILES * SQ]).then_inc(S["unloaded_even"], 1)
                            if st.has_next(u):
                                t, part = divmod(s - L.per - 3, L.per)
                                if L.rope and 0 <= t < L.nt and part == 0:
                                    shuffle(st, ("K", u, t))
                                t, part = divmod(s - L.per - (5 if L.rope else L.k_parts + 1), L.per)
                                if 0 <= t < L.nt and part == 0:
                                    split(st, ("K", u, t))
                            if L.rope and (u == 1 or not st.begin):
                                if s == 3:
                                    finish(st, u - 1)
                                if s == 6:
                                    post(st, u - 1)
                            if L.ctx_norm and st.has_after(u):
                                if 1 <= s <= KV_TILES:
                                    context_stats(st, u, s - 1)
                                if s == 4:
                                    moments(st, ("ctx", u), KV_ROWS, 0)
                            if st.has_pair(u):
                                if L.x_norm:
                                    if s in (5, 6):
                                        stats(SQ, x_rows(st, s - 5), s - 1, end=s == 6)
                                    if s == 7:
                                        moments(st, ("x", u), [SQ, SQ], 4)
                                    if s in (14, 15):
                                        x_norm(st, u, s - 14)
                                elif s in (7, 8):
                                    x_copy(st, u, s - 7)
                            if s == H + 1:
                                invert(st, u)

                    def invert(st, u):
                        dve.wait_ge(S["exped"], st.head(u, H - 1) + 2)
                        nc.vector.reciprocal(RDEN[:, :], DEN[:, u, :]).then_inc(S["inverse"], 1)
                        dve.wait_ge(S["inverse"], st.batch(u) + 1)
                        nc.vector.tensor_copy(RX[:, 0:L.hw].rearrange("p (h r) -> p h r", h=H),
                                              RDEN[:, :].unsqueeze(2).to_broadcast([SQ, H, L.rows])).then_inc(S["repeated"], 1)

                    def scale(st, u):
                        for r in range(L.nr):
                            dve.wait_ge(S["taken"], st.jobs.upto(("R", u, r)))
                            o = OT[:, 4 * r:4 * r + 4, :].rearrange("p t q -> p (t q)")
                            nc.vector.tensor_tensor(o, PO[r][:, 0:4 * SQ], o, ALU.mult).then_inc(S["freed"], 1)
                        dve.wait_ge(S["freed"], (st.batch(u) + 2) * L.nr)
                        dve.sem_inc(S["scaled"], 1)

                    def finish(st, u):
                        n = st.batch(u)
                        x = X[:, n, :]
                        dve.wait_ge(S["taken"], st.jobs.upto_or_before(("out", u, 0)))
                        nc.vector.tensor_tensor(x, x, Y[:, :], ALU.add).then_inc(S["added"], 1)
                        wait_apart(dve, S["added"], n + 1)
                        stats(SQ, x, 3, end=True)
                        moments(st, ("post", u), [SQ], 3)

                    def post(st, u):
                        n = st.batch(u)
                        x = X[:, n, :]
                        dve.wait_ge(S["rstd"], st.norms.upto_or_before(("post", u)))
                        nc.vector.tensor_scalar(Y[:, :], x, MV[0:SQ, 3, 0:1], RS[0:SQ, 3:4], ALU.subtract, ALU.mult).then_inc(S["normed"], 1)
                        dve.wait_ge(S["normed"], st.norms.upto_or_before(("post", u)))
                        nc.vector.tensor_tensor(Y[:, :], Y[:, :], ROWS[:, 2, :], ALU.mult).then_inc(S["gammaed"], 1)
                        dve.wait_ge(S["gammaed"], n + 1)
                        nc.vector.tensor_tensor(x, Y[:, :], ROWS[:, 3, :], ALU.add).then_inc(S["summed"], 1)

                    st = Stage(L, -1)
                    def context_whole(st, u):
                        for t in range(KV_TILES):
                            context_stats(st, u, t)
                        moments(st, ("ctx", u), KV_ROWS, 0)

                    if L.ctx_norm:
                        context_whole(st, -2)
                        first_norm(st)
                    for v in range(2):
                        if L.x_norm:
                            stats(SQ, x_rows(st, v), 4 + v, end=v == 1)
                        else:
                            x_copy(st, -1, v)
                    if L.x_norm:
                        moments(st, ("x", -1), [SQ, SQ], 4)
                        for v in range(2):
                            x_norm(st, -1, v)
                    split_low(0)
                    splits(st, [("ctx", -2, k) for k in range(KE)])
                    splits(st, [("xT", -1, k) for k in range(KE)])
                    split_low(1)
                    split_low(2)
                    splits(st, [("K", -1, t) for t in range(L.nt)])
                    if L.ctx_norm:
                        context_whole(st, -1)
                    splits(st, [("Q", -1, t) for t in range(L.nt)])
                    splits(st, [("ctx", -1, k) for k in range(KE)])
                    if not L.wide:
                        for t in range(L.nt):
                            last = nc.vector.tensor_scalar(OT[:, t, :], ident[:, 0:SQ], 0.0, col(nm + "bv", t), ALU.mult, ALU.add)
                        last.then_inc(S["bias_spread"], 1)
                    for h in range(LEAD):
                        maximum(st, 2, h)
                    if not L.wide:
                        row = ROWS[:, out_bias, :]
                        if ph == 0:
                            dve.wait_ge(s_rows, 16 * len(row_src))
                        dve.wait_ge(S["bias_made"], 1)
                        nc.vector.tensor_tensor(row, row, PO[0][0:SQ, 0:E], ALU.add)

                    def body(st):
                        for u in range(2):
                            heads(st, u)
                            if st.has_pair(u):
                                splits(st, [("xT", u, k) for k in range(KE)])
                                early = [k for k in st.tail(u)[:st.tail(u).index(("R", u, 0))] if k[0] == "Q"]
                                splits(st, early)
                            scale(st, u)
                            if st.has_pair(u) and len(early) < L.nt:
                                splits(st, [("Q", u, t) for t in range(len(early), L.nt)])
                            for k in range(KE):
                                if st.has_after(u):
                                    split(st, ("ctx", u, k))
                                if st.has_next(u):
                                    maximum(st, u + 1, k)
                    if not L.rope:
                        loop(dve, body)
                    else:
                        body(Stage(L, 0))
                        with dve.Fori(1, PAIRS - 1) as i:
                            body(Stage(L, i))
                        st = Stage(L, PAIRS - 1, last=True)
                        body(st)
                        finish(st, 1)
                        post(st, 1)

                @block.gpsimd
                def _(pool):
                    if not L.rope:
                        pool.sem_inc(S["summed"], 1)
                    if not L.wide:
                        nc.gpsimd.memset(WO[:, 0:4 * E], 0.0).then_inc(S["cleared_w"], 1)
                        nc.gpsimd.memset(V[:, 0:KV_TILES * L.hw], 0.0).then_inc(S["cleared_v"], 1)

                    def rstd(st, key, at, n, eps):
                        m = st.norms.upto(key)
                        wait_apart(pool, S["moments"], m)
                        ve, mean, var = VE[:, at:at + n], MV[:, at:at + n, 0], MV[:, at:at + n, 1]
                        if nm == "L1":
                            nc.gpsimd.tensor_tensor(ve, mean, mean, ALU.mult).then_inc(S["square"], 1)
                            pool.wait_ge(S["square"], m)
                            nc.gpsimd.tensor_tensor(SQV[:, at:at + n], ve, var, ALU.add).then_inc(S["squares"], 1)
                            wait_apart(pool, S["squares"], m)
                            var = SQV[:, at:at + n]
                        nc.gpsimd.tensor_scalar(EV[:, at:at + n], var, eps, None, ALU.add).then_inc(S["powers"], 1)
                        pool.wait_ge(S["powers"], m)
                        nc.gpsimd.tensor_tensor(RS[:, at:at + n], EV[:, at:at + n], HALF[:, at:at + n], ALU.pow).then_inc(S["rstd"], 1)

                    def context_norm(st, u):
                        n, m = u % 2, st.norms.upto(("ctx", u))
                        wait_apart(pool, S["rstd"], m)
                        if st.first and u == -1:
                            pool.wait_ge(S["product"], st.jobs.upto(("ctx", -2, KE - 1)))
                        for t, r in enumerate(KV_ROWS):
                            last = nc.gpsimd.tensor_scalar(CN[0:r, t, :], C[0:r, n, t, :], MV[0:r, t, 0:1], RS[0:r, t:t + 1], ALU.subtract, ALU.mult)
                        last.then_inc(S["normed"], 1)

                    def tables(st, u):
                        slot = u % 2
                        n = u + 3 if st.first else st.batch(u) + 3
                        wait_apart(pool, s_m[slot], 16 if st.first else st.i * 16 + 32)
                        nc.gpsimd.tensor_copy(MF[:, :], M8[:, slot, :]).then_inc(S["mask_float"], 1)
                        wait_apart(pool, S["mask_float"], n)
                        nc.gpsimd.tensor_tensor(COSM[:, :], cos, MF[:, :], ALU.mult)
                        nc.gpsimd.tensor_tensor(SINM[:, :], sin, MF[:, :], ALU.mult)
                        nc.gpsimd.tensor_scalar(MNEG[:, slot, :], MF[:, :], -1.0, None, ALU.add).then_inc(S["mask_tables"], 1)
                        wait_apart(pool, S["mask_tables"], n)

                    def rotate(st, todo):
                        for key in todo:
                            r, slot, keys = st.turns.upto(key), st.turns.slot(key), key[0] == "K"
                            src = T32[:, st.splits.slot(key), 0:SKE if keys else 2 * SQ]
                            ac, sh, c, s = AC[:, slot, :], SH[:, slot, :], COSM[:, :], SINM[:, :]
                            if not keys:
                                src, ac, sh = [x[:, 0:2 * SQ].rearrange("p (v q) -> p v q", v=2) for x in (src, ac, sh)]
                                c, s = [x[:, 0:SQ].unsqueeze(1).to_broadcast([128, 2, SQ]) for x in (cos, sin)]
                            pool.wait_ge(S["shuffled"], r)
                            nc.gpsimd.tensor_tensor(ac, src, c, ALU.mult)
                            nc.gpsimd.tensor_tensor(sh, sh, s, ALU.mult).then_inc(S["rotated"], 1)

                    def stand_alone(st, u):
                        for v in range(2):
                            for t in range(L.nt):
                                pool.wait_ge(S["split"], st.splits.upto(("Q", u, t)))
                                for Q_, A in zip((QH, QL), QA):
                                    last = nc.gpsimd.tensor_tensor(A[:, v, 4 * t:4 * t + 4, :],
                                                                   Q_[:, t, SQ * v:SQ * v + SQ].bitcast(fp32).unsqueeze(1).to_broadcast([128, 4, SQ]),
                                                                   own.unsqueeze(2).to_broadcast([128, 4, SQ]), ALU.mult)
                                last.then_inc(S["masked"], 1)

                    def finish(st, u):
                        n = st.batch(u)
                        x = X[:, n, :]
                        wait_apart(pool, S["taken"], st.jobs.upto(("out", u, 0)))
                        last = nc.gpsimd.tensor_tensor(x, x, Y[:, :], ALU.add)
                        if nm != "L1":
                            last.then_inc(S["added"], 1)
                            wait_apart(pool, S["added"], n + 1)
                            last = nc.gpsimd.tensor_tensor(x, x, ROWS[:, out_bias, :], ALU.add)
                        last.then_inc(S["summed"], 1)

                    def segment(st, u):
                        if L.ctx_norm and st.has_after(u):
                            rstd(st, ("ctx", -2 if st.first else u), 0, KV_TILES, L.eps)
                            if not st.first:
                                context_norm(st, u)
                        if L.x_norm and st.has_pair(u):
                            rstd(st, ("x", u), 4, 2, L.eps)
                        if L.ctx_norm and st.first:
                            rstd(st, ("ctx", u), 0, KV_TILES, L.eps)
                            context_norm(st, u)
                        if L.rope and st.first:
                            tables(st, -2)
                        if L.rope and u == 1:
                            rstd(st, ("post", 0), 3, 1, L.eps_post)
                        if L.rope and st.has_next(u):
                            rotate(st, [("K", u, t) for t in range(L.nt)])
                        if L.rope and st.has_pair(u):
                            rotate(st, [("Q", u, t) for t in range(L.nt)])
                        if L.rope and st.has_after(u):
                            tables(st, u)
                        if L.eps_post is not None and u == 1:
                            rstd(st, ("post", u), 3, 1, L.eps_post)

                        if not L.wide and st.has_pair(u):
                            stand_alone(st, u)
                        if not L.rope and not st.first:
                            finish(st, u)

                    segment(Stage(L, -1), -1)

                    def body(st):
                        for u in range(2):
                            segment(st, u)
                    loop(pool, body)

        def feed_forward():
            G = 4
            groups = B // G
            nf = FF // 128
            YN = RX[:, :].rearrange("p (g e) -> p g e", g=G)
            YH, YL = [K_[:, :, :].rearrange("p t n -> p (t n)")[:, 0:KE * G * SQ].rearrange("p (k n) -> p k n", k=KE) for K_ in (KH, KL)]
            HT = V[:, 0:nf * G * SQ].rearrange("p (t n) -> p t n", t=nf)
            banks = [*PJ, *PS_, *PP, PO[0]]
            nb = len(banks)
            HID, TURN, OUT = KE, KE + nf, KE + nf + KE
            per = nf + KE + G
            assert per % nb == 0

            def loop(eng, body):
                with eng.Fori(0, groups - 1) as i:
                    body(i, False)
                body(groups - 1, True)

            with nc.Block() as block:

                @block.sync
                def _(sp):
                    load_output_weights(sp, "ffn")
                    sp.wait_ge(S["low_w"], 1)
                    load_weights(sp, "L1")

                @block.tensor
                def _(pe):
                    pe.sem_inc(S["taken"], nb)

                    def begin(i, n):
                        pe.wait_ge(S["taken"], i * per + (n + 1))
                        return banks[n % nb]

                    def turn(i, n0, group):
                        pe.wait_ge(S["normed"], group + 1)
                        for k in range(KE):
                            bank = begin(i, n0 + k)
                            for g in range(G):
                                last = nc.tensor.transpose(bank[:, SQ * g:SQ * g + SQ], YN[:, g, 128 * k:128 * k + 128], ident[0:SQ, 0:SQ])
                            last.then_inc(S["product"], 1)

                    turn(0, 0, 0)
                    pe.wait_ge(S["low_w"], 1)

                    def body(i, last_group):
                        pe.wait_ge(S["split"], i * KE + KE)
                        for t in range(nf):
                            bank = begin(i, HID + t)
                            todo = [x for k in range(KE) for lh, ll in [[W[:, FF * k + 128 * t:FF * k + 128 * t + 128] for W in (WH, WL)]]
                                    for x in ((lh, YH[:, k, :]), (lh, YL[:, k, :]), (ll, YH[:, k, :]))]
                            for m, (x, y) in enumerate(todo):
                                last = nc.tensor.matmul(bank[:, 0:G * SQ], x, y, start=m == 0, stop=m == len(todo) - 1)
                            last.then_inc(S["product"], 1)
                        if not last_group:
                            turn(i, TURN, i + 1)
                        pe.wait_ge(wo_in["ffn"], 16)
                        pe.wait_ge(S["taken"], i * per + (HID + nf + nb))
                        for g in range(G):
                            bank = begin(i, (TURN if last_group else OUT) + g)
                            for t in range(nf):
                                last = nc.tensor.matmul(bank[0:SQ, 0:E], HT[:, t, SQ * g:SQ * g + SQ], WO[:, E * t:E * t + E],
                                                        start=t == 0, stop=t == nf - 1)
                            last.then_inc(S["product"], 1)
                    loop(pe, body)

                @block.scalar
                def _(act):
                    act.wait_ge(w_in["ffn"][0], 16)
                    nc.scalar.activation(WH[:, 0:KE * FF], W_RAW[:, 0, :], ACT.Copy).then_inc(S["high_w"], 1)

                    def gain(i, n0):
                        for k in range(KE):
                            act.wait_ge(S["product"], i * per + (n0 + k + 1))
                            nc.scalar.activation(T32[:, k, :], banks[(n0 + k) % nb][:, 0:G * SQ], ACT.Identity, bias=col("b2n", k),
                                                 scale=col("g2", k)).then_inc(S["taken"], 1)

                    gain(0, 0)

                    def body(i, last_group):
                        for t in range(nf):
                            act.wait_ge(S["product"], i * per + (HID + t + 1))
                            nc.scalar.activation(HT[:, t, :], banks[(HID + t) % nb][:, 0:G * SQ], ACT.Gelu, bias=col("b1", t)).then_inc(S["taken"], 1)
                        if not last_group:
                            gain(i, TURN)
                        act.wait_ge(S["summed"], i * G + 1)
                        for g in range(G):
                            n = (TURN if last_group else OUT) + g
                            act.wait_ge(S["product"], i * per + (n + 1))
                            nc.scalar.activation(P[:, g, 0:E], banks[n % nb][0:SQ, 0:E], ACT.Copy).then_inc(S["taken"], 1)
                    loop(act, body)

                @block.vector
                def _(dve):
                    dve.sem_inc(S["summed"], 1)
                    dve.wait_ge(S["high_w"], 1)
                    nc.vector.tensor_tensor(WL[:, 0:KE * FF], W_RAW[:, 0, :], WH[:, 0:KE * FF].bitcast(fp32), ALU.subtract).then_inc(S["low_w"], 1)

                    def normalise(group):
                        rows = [X[:, group * G + g, :] for g in range(G)]
                        for g in range(G):
                            last = nc.vector.bn_stats(BN[0:SQ, g, :], rows[g])
                        last.then_inc(S["stats"], 1)
                        wait_apart(dve, S["stats"], group + 1)
                        for g in range(G):
                            last = nc.vector.bn_aggr(MV[0:SQ, g, :], BN[0:SQ, g, :])
                        last.then_inc(S["moments"], 1)
                        dve.wait_ge(S["rstd"], group + 1)
                        for g in range(G):
                            last = nc.vector.tensor_scalar(YN[:, g, :], rows[g], MV[0:SQ, g, 0:1], RS[0:SQ, g:g + 1], ALU.subtract, ALU.mult)
                        last.then_inc(S["normed"], 1)

                    def split(i, n0, group):
                        for k in range(KE):
                            dve.wait_ge(S["taken"], i * per + (n0 + k + 1 + nb))
                            nc.vector.tensor_copy(YH[:, k, :], T32[:, k, :]).then_inc(S["rounded"], 1)
                            dve.wait_ge(S["rounded"], group * KE + (k + 1))
                            nc.vector.tensor_tensor(YL[:, k, :], T32[:, k, :], YH[:, k, :].bitcast(fp32), ALU.subtract).then_inc(S["split"], 1)

                    normalise(0)
                    split(0, 0, 0)

                    def body(i, last_group):
                        if not last_group:
                            normalise(i + 1)
                            split(i, TURN, i + 1)
                        for g in range(G):
                            x = X[:, i * G + g, :]
                            dve.wait_ge(S["taken"], i * per + ((TURN if last_group else OUT) + g + 1 + nb))
                            nc.vector.tensor_tensor(x, x, P[:, g, 0:E], ALU.add).then_inc(S["added"], 1)
                            dve.wait_ge(S["added"], i * G + (g + 1))
                            nc.vector.tensor_tensor(x, x, ROWS[:, 1, :], ALU.add).then_inc(S["summed"], 1)
                    loop(dve, body)

                @block.gpsimd
                def _(pool):
                    def rstd(group):
                        wait_apart(pool, S["moments"], group + 1)
                        nc.gpsimd.tensor_scalar(EV[:, 0:G], MV[:, 0:G, 1], 1e-5, None, ALU.add).then_inc(S["powers"], 1)
                        pool.wait_ge(S["powers"], group + 1)
                        nc.gpsimd.tensor_tensor(RS[:, 0:G], EV[:, 0:G], HALF[:, 0:G], ALU.pow).then_inc(S["rstd"], 1)

                    rstd(0)
                    with pool.Fori(0, groups - 1) as i:
                        rstd(i + 1)

        for ph, what in enumerate(PHASES):
            if ph:
                clear_semaphores()
            if what == "ffn":
                feed_forward()
            else:
                attention(what, ph)


def constants():
    import numpy as np
    c = np.zeros((128, C_END), np.float32)
    c[:, C_ID:C_ID + 128] = np.eye(128)
    d = np.arange(128) % 64
    inv = (1.0 / np.float32(10000.0) ** (((d // 2) * 2).astype(np.float32) / np.float32(64))).astype(np.float32)
    ang = (np.arange(SKE, dtype=np.float32)[None, :] * inv[:, None]).astype(np.float32).astype(np.float64)
    c[:, C_COS:C_COS + SKE] = np.cos(ang)
    c[:, C_SIN:C_SIN + SKE] = np.sin(ang) * np.where(d % 2 == 0, -1.0, 1.0)[:, None]
    c[np.arange(128), C_OWN + np.arange(128) // 32] = 1.0
    c[:, C_NEG] = np.where(np.arange(128) % 32 >= 16, -1.0, 0.0)
    high = float(int(NEG) >> 18 << 18)
    c[0, C_FILL:C_FILL + SQ], c[1, C_FILL:C_FILL + SQ] = high, NEG - high
    return c


def vectors(a):
    import numpy as np
    out = np.zeros((128, VEC_END), np.float32)

    def tiles(name, src):
        v = np.asarray(a[src]).reshape(-1, 128)
        for k in range(v.shape[0]):
            out[:, VEC_COLS[name] + k] = v[k]
    for p, names in (("L0", ("ln1_g", "ln1_b", "ln1_g", "ln1_b")), ("L3", ("gkv", "betakv", "gq", "betaq"))):
        for v, src in zip(("cg", "cb", "xg", "xb"), names):
            tiles(p + v, f"{p}_xattn_{src}")
        for v in ("bq", "bk", "bv"):
            h = np.asarray(a[f"{p}_xattn_{v}"]).reshape(4, 4, 16)
            for t in range(4):
                for g in range(4):
                    for twice in range(1 if v == "bv" else 2):
                        r = 32 * g + 16 * twice
                        out[r:r + 16, VEC_COLS[p + v] + t] = h[t, g]
    for v, src in (("g2", "L0_xattn_ln2_g"), ("b2n", "L0_xattn_ln2_b"), ("b1", "L0_xattn_b1"), ("nw", "L1_xattn_norm_w")):
        tiles(v, src)
    return out


def kernel(**inputs):
    import numpy as np
    import concourse.bacc as bacc
    from concourse.bass_utils import run_bass_kernel_spmd

    nc = bacc.Bacc("TRN2", target_bir_lowering=False, num_devices=1)
    arrays, args = {}, {}
    for name, value in inputs.items():
        v = np.ascontiguousarray(value)
        short = "mask" if name == "mask_BxS2_bf1" else name
        if short == "mask":
            v = v.view(np.uint8)
        arrays[f"in_{short}"] = v
        args[short] = nc.dram_tensor(f"in_{short}", v.shape, mybir.dt.from_np(v.dtype), kind="ExternalInput").ap()
    arrays["vectors"] = vectors(inputs)
    args["vectors"] = nc.dram_tensor("vectors", (128, VEC_END), fp32, kind="ExternalInput").ap()
    arrays["constants"] = constants()
    consts = nc.dram_tensor("constants", (128, C_END), fp32, kind="ExternalInput").ap()
    out = nc.dram_tensor("out", (B, SQ, E), fp32, kind="ExternalOutput").ap()
    build(nc, args, consts, out)
    r = run_bass_kernel_spmd(nc, [{**arrays}], core_ids=[0])
    return r.results[0]["out"]
```
